# Optimizing a Trainium2 kernel written in Bass

```python
import numpy as np
import jax
import jax.numpy as jnp

def _softmax(x, axis=-1):
    return jax.nn.softmax(x, axis=axis)
def _gelu(x):
    return jax.nn.gelu(x, approximate=True)
def _silu(x):
    return jax.nn.silu(x)
def _sigmoid(x):
    return jax.nn.sigmoid(x)
def _layernorm(x, axis=-1, eps=1e-5):
    m = jnp.mean(x, axis=axis, keepdims=True)
    v = jnp.var(x, axis=axis, keepdims=True)
    return (x - m) / jnp.sqrt(v + eps)
def _scatter_add(tgt, idx, src, axis=0):
    return tgt.at[idx].add(src)
def _segment_sum(src, seg, n):
    return jax.ops.segment_sum(src, seg, n)

kernel_name = 'mk_conv_preact_d2_conv_nhwc32_3b29c3'

def setup_inputs(seed: int = 0):
    np.random.seed(seed)
    _w = jnp.asarray
    def _rec_inputs():
        import jax
        import jax.numpy as jnp
        _gk = jax.random.key(seed)
        x = -7.109e-05 + 0.9999 * jax.random.normal(jax.random.fold_in(_gk, 1), (8, 512, 512, 32), jnp.float32)
        return x
    x = _rec_inputs()
    def _L0_conv_setup():
        import jax, jax.numpy as jnp
        import numpy as np
        B, H, Wd, C = (8, 512, 512, 32)
        MODES = 32
        key = jax.random.key(seed)
        k1, k2 = jax.random.split(key)
        x = jax.random.normal(k1, (B, H, Wd, C), dtype=jnp.float32)
        scale = (2.0 / (C + C)) ** 0.5
        W = jax.random.normal(k2, (MODES, MODES, C, C), dtype=jnp.float32) * scale
        return {'x': x, 'W': W}
    _L0_conv_all = _L0_conv_setup()
    _L0_conv_in = {k: v for k, v in _L0_conv_all.items() if k in ('W', )}
    del _L0_conv_all

    def _L1_conv_setup():
        import jax, jax.numpy as jnp
        import numpy as np
        from jax import lax
        K = 5
        PAD = K - 1
        PAD_L = PAD // 2
        PAD_R = PAD - PAD_L

        def _mvcnn_down(inputs, w, b):
            kernel = jnp.transpose(w[:, :, 0, :], (1, 0, 2))

            def conv_row(x):
                return lax.conv_general_dilated(x, kernel, window_strides=(1,), padding=[(PAD_L, PAD_R)], dimension_numbers=('NWC', 'WIO', 'NWC'))
            rows = jnp.transpose(inputs, (1, 0, 2, 3))

            def step(carry, row):
                x = row + carry
                r = jax.nn.relu(conv_row(x) + b)
                return (r, r)
            init = jnp.zeros_like(rows[0])
            _, out_rows = lax.scan(step, init, rows)
            return jnp.transpose(out_rows, (1, 0, 2, 3))
        key = jax.random.key(seed)
        k1, k2 = jax.random.split(key)
        B, H, W, C = (16, 256, 256, 32)
        inputs = jax.random.normal(k1, (B, H, W, C), dtype=jnp.float32)
        w = jax.random.normal(k2, (C, K, 1, C), dtype=jnp.float32) * 0.05
        b = jnp.zeros((C,), dtype=jnp.float32)
        return {'inputs': inputs, 'w': w, 'b': b}
    _L1_conv_all = _L1_conv_setup()
    _L1_conv_in = {k: v for k, v in _L1_conv_all.items() if k in ('w', 'b', )}
    del _L1_conv_all

    return {
        "x": x,
        "L0_conv_W": _L0_conv_in["W"],
        "L1_conv_w": _L1_conv_in["w"],
        "L1_conv_b": _L1_conv_in["b"],
    }

def reference(x, L0_conv_W, L1_conv_w, L1_conv_b):
    import jax
    import jax.numpy as jnp
    def _L0_conv_ref(x, W):
        import jax, jax.numpy as jnp
        import numpy as np
        B, H, Wd, C = (8, 512, 512, 32)
        MODES = 32
        modes = W.shape[0]
        h, w = (x.shape[1], x.shape[2])
        xf = jnp.fft.rfft2(x, axes=(1, 2))
        low = xf[:, :modes, :modes, :]
        out_low = jnp.einsum('bxyc,xycd->bxyd', low, W.astype(xf.dtype))
        out_f = jnp.pad(out_low, ((0, 0), (0, xf.shape[1] - modes), (0, xf.shape[2] - modes), (0, 0)))
        return jnp.fft.irfft2(out_f, s=(h, w), axes=(1, 2))

    def _L1_conv_ref(inputs, w, b):
        import jax, jax.numpy as jnp
        import numpy as np
        from jax import lax
        K = 5
        PAD = K - 1
        PAD_L = PAD // 2
        PAD_R = PAD - PAD_L

        def _mvcnn_down(inputs, w, b):
            kernel = jnp.transpose(w[:, :, 0, :], (1, 0, 2))

            def conv_row(x):
                return lax.conv_general_dilated(x, kernel, window_strides=(1,), padding=[(PAD_L, PAD_R)], dimension_numbers=('NWC', 'WIO', 'NWC'))
            rows = jnp.transpose(inputs, (1, 0, 2, 3))

            def step(carry, row):
                x = row + carry
                r = jax.nn.relu(conv_row(x) + b)
                return (r, r)
            init = jnp.zeros_like(rows[0])
            _, out_rows = lax.scan(step, init, rows)
            return jnp.transpose(out_rows, (1, 0, 2, 3))
        return _mvcnn_down(inputs, w, b)

    def _gn(v, G=16, eps=1e-5):
        B_, H_, W_, C_ = v.shape
        g = v.reshape(B_, H_, W_, G, C_ // G)
        m = jnp.mean(g, axis=(1, 2, 4), keepdims=True)
        s = jnp.var(g, axis=(1, 2, 4), keepdims=True)
        return ((g - m) / jnp.sqrt(s + eps)).reshape(v.shape)

    def _ln_c(v, eps=1e-6):
        m = jnp.mean(v, axis=-1, keepdims=True)
        s = jnp.var(v, axis=-1, keepdims=True)
        return (v - m) / jnp.sqrt(s + eps)

    def _ln_t(v, eps=1e-5):
        m = jnp.mean(v, axis=-1, keepdims=True)
        s = jnp.var(v, axis=-1, keepdims=True)
        return (v - m) / jnp.sqrt(s + eps)

    def _to_tokens(v):
        B_, H_, W_, C_ = v.shape
        return v.reshape(B_, H_ * W_, C_)
    def _from_tokens(t, like):
        return t.reshape(like.shape)

    x = x + _L0_conv_ref(_gn(x), L0_conv_W)
    x = x + _L1_conv_ref(_gn(x), L1_conv_w, L1_conv_b)
    return x


_drawn_inputs = setup_inputs


def setup_inputs(seed=0):
    import zlib

    import numpy as np

    out = dict(_drawn_inputs(seed))
    spreads = {'L1_conv_b': (0.0, 0.1)}
    factors = {}
    for name, (base, spread) in spreads.items():
        noise = np.random.default_rng([zlib.crc32(name.encode()), seed]).standard_normal(out[name].shape)
        drawn = base * np.exp(spread * noise) if base else spread * noise
        out[name] = jnp.asarray(drawn.astype(out[name].dtype))
    for name, factor in factors.items():
        out[name] = (out[name] * factor).astype(out[name].dtype)
    return out
```

```python
from contextlib import ExitStack

import concourse.bass as bass
import numpy as np
from concourse import mybir

F32 = mybir.dt.float32
ALU = mybir.AluOpType
ACT = mybir.ActivationFunctionType
AX = mybir.AxisListType

P = 128
BANK = 512
M = 32
GN_EPS = 1e-5


def table_layout(H):
    sizes = [("dft_h", H // P * 64), ("dft_w", 2 * 4 * 64), ("idft_h", H), ("idft_w", 2 * 4 * P),
             ("ident", P), ("ones", P), ("dc", P), ("cross", P), ("power", P), ("power0", P),
             ("same_group16", 16), ("same_group32", 32)]
    at, cols = 0, {}
    for name, n in sizes:
        cols[name] = (at, n)
        at += n
    return cols, at


def tables(H, W):
    cols, total = table_layout(H)
    out = np.zeros((P, total))

    def put(name, rows, values):
        at, n = cols[name]
        out[rows, at:at + n] = values.reshape(values.shape[0], n)

    every = slice(0, P)
    p, k = np.arange(P), np.arange(M)
    h = (np.arange(H // P)[None, :] * P + p[:, None])[:, :, None] * k * (2 * np.pi / H)
    put("dft_h", every, np.concatenate([np.cos(h), np.sin(h)], -1))
    w = (np.arange(4)[None, :] * P + p[:, None])[:, :, None] * k * (2 * np.pi / W)
    put("dft_w", every, np.stack([np.concatenate([np.cos(w), -np.sin(w)], -1),
                                  np.concatenate([-np.sin(w), -np.cos(w)], -1)], 1))
    a = k[:, None] * np.arange(H) * (2 * np.pi / H)
    put("idft_h", every, np.concatenate([np.cos(a), np.sin(a)] * 2, 0))
    N = H * W
    twice = np.where(k == 0, 1.0, 2.0)
    pos = 4 * np.arange(P)[None, :] + np.arange(4)[:, None]
    a = k[:, None, None] * pos * (2 * np.pi / W)
    t = twice[:, None, None] / N * np.stack([np.cos(a), -np.sin(a)])
    t = t.reshape(64, 4 * P)
    z = np.zeros_like(t)
    put("idft_w", every, np.concatenate([np.concatenate([t, z], 1), np.concatenate([z, t], 1)], 0))
    put("ident", every, np.eye(P))
    put("ones", every, np.ones((P, P)))
    rows = slice(0, 64)
    wide = np.ones((1, P))
    dc = np.zeros((64, 1))
    dc[0] = 1
    put("dc", rows, dc * wide)
    put("cross", rows, np.tile(2 * twice / N, 2)[:, None] * wide)
    put("power", rows, np.tile(np.where(k == 0, 0.5, 2.0) / N, 2)[:, None] * wide)
    p0 = np.zeros((64, 1))
    p0[0], p0[M] = 0.5 / N, -0.5 / N
    put("power0", rows, p0 * wide)
    group = (p % 32) // 2
    put("same_group16", every, (group[:, None] == np.arange(16)).astype(float))
    put("same_group32", every, (group[:, None] == np.arange(32) // 2).astype(float))
    return out.astype(np.float32)


def conv_preact_pair(nc, x, spec_w, conv_w, conv_b, tab, out):
    B, H, W, C = x.shape
    assert (B, W, C) == (8, 512, 32) and H % P == 0
    HH = H // P
    G = 2
    BG = B // G
    ROW = W * C
    TW = 32
    TILES = W // 2 // TW
    TILE = 2 * TW * C
    SQ_ACT = 10
    SQ_DVE = 16 - SQ_ACT
    CH = 4
    CHUNKS = H // CH
    STEPS = 16
    N2 = float(2 * H * W)

    x_tiles = x.rearrange("b (hh p) (half i w) c -> b i hh p half (w c)", p=P, half=2, i=TILES)
    x_rows = x.rearrange("b h (j q) c -> b j h (q c)", q=4)
    out_rows = out.rearrange("b h (j q) c -> b j h (q c)", q=4)
    X_dram = nc.dram_tensor("modes_in", (B, 64, C, M), F32, kind="Internal").ap()
    O_dram = nc.dram_tensor("modes_out", (2 * B, M, M, C), F32, kind="Internal").ap()
    V_dram = nc.dram_tensor("row_spectra", (CHUNKS, 64, B, CH * C), F32, kind="Internal").ap()

    ctx = ExitStack()
    with ctx:
        def sb(name, cols):
            return ctx.enter_context(nc.sbuf_tensor(name, [P, cols], F32))

        def sem(name):
            return ctx.enter_context(nc.semaphore(name))

        cols, total = table_layout(H)
        T = sb("tables", total)

        def table(name, lo=0, hi=P):
            at, n = cols[name]
            return T[lo:hi, at:at + n]

        KB = 256
        arena = sb("arena", 164 * KB)

        def region(kb, size_kb):
            return arena[:, kb * KB:(kb + size_kb) * KB]

        tile = [region(32 * s, 8 * HH).rearrange("p (hh n) -> p hh n", hh=HH) for s in range(2)]
        Z = region(64, 32).rearrange("p (c w) -> p c w", c=C)
        ZT = [region(96 + 16 * s, 16).rearrange("p (c k) -> p c k", c=C) for s in range(2)]
        X = region(128, 32).rearrange("p (b n) -> p b n", b=B)
        sq = sb("sq", B * TILES * 16)
        SQ = TILE * HH // 16
        squares_act = [region(160 + 2 * s, 2)[:, 0:SQ].rearrange("p (w c) -> p w c", c=2) for s in range(2)]
        squares_dve = [sb(f"squares_dve{s}", SQ).rearrange("p (w c) -> p w c", c=2) for s in range(2)]
        spec = region(0, 32)
        O_part = region(32, 32)
        XC = region(64, 16).rearrange("p (r n) -> p r n", r=2 * B)
        O = region(96, 32).rearrange("p (b n) -> p b n", b=B)
        LV = [region(16 * s, 16).rearrange("p (m d) -> p m d", d=C) for s in range(2)]
        VH = H // 2
        VS = [region(32 + 32 * s, H // 16).rearrange("p (h d) -> p h d", d=C) for s in range(2)]
        prod = region(160, 4)
        x_in = [region(16 * s, 16).rearrange("p (b h n) -> p b h n", b=B, h=CH) for s in range(2)]
        x1 = [region(32 + 16 * s, 16).rearrange("p (b h n) -> p b h n", b=B, h=CH) for s in range(4)]
        gx = [region(96 + 16 * s, 16).rearrange("p (b h n) -> p b h n", b=B, h=CH) for s in range(2)]
        Vc = [region(128 + 2 * s, 2) for s in range(2)]
        r = [[region(132 + 4 * g + 2 * s, 2) for s in range(2)] for g in range(G)]
        u = [arena[:, 140 * KB + g * BG * 130:140 * KB + (g + 1) * BG * 130]
             .rearrange("p (b j) -> p b j", b=BG) for g in range(G)]
        conv = sb("conv_w", 4 * 64).rearrange("p (m n) -> p m n", m=4)
        bias, neg_bias = sb("bias", 1), sb("neg_bias", 1)
        small = sb("small", 16 * B).rearrange("p (n b) -> p n b", b=B)
        sumsq = sb("sumsq", 16 * B)
        masked = sb("masked", C * B)
        R1, R2, R3 = sb("R1", C * B), sb("R2", C * B), sb("R3", C * B)
        ps = [ctx.enter_context(nc.psum_tensor(f"ps{i}", [P, BANK], F32)) for i in range(8)]

        tables_in, bias_in, conv_in = sem("tables_in"), sem("bias_in"), sem("conv_in")
        conv_zero, spec_in = sem("conv_zero"), sem("spec_in")
        tile_in = [sem(f"tile_in{s}") for s in range(2)]
        sq_act, sq_dve, squared = sem("sq_act"), sem("sq_dve"), sem("squared")
        rowdft_done, z_copied = sem("rowdft_done"), sem("z_copied")
        zt_done, zt_copied = sem("zt_done"), sem("zt_copied")
        coldft_done, x_copied, x_stored = sem("coldft_done"), sem("x_copied"), sem("x_stored")
        xc_in, xc_scaled = sem("xc_in"), sem("xc_scaled")
        dve_step, sums_ready, sums_done = sem("dve_step"), sem("sums_ready"), sem("sums_done")
        var_ready, root_done = sem("var_ready"), sem("root_done")
        mix_done, o_copied, o_stored = sem("mix_done"), sem("o_copied"), sem("o_stored")
        o_in, lv_zero, lv_signed = sem("o_in"), sem("lv_zero"), sem("lv_signed")
        lv_in = [sem(f"lv_in{s}") for s in range(2)]
        v_done, v_copied_act, v_copied_dve = sem("v_done"), sem("v_copied_act"), sem("v_copied_dve")
        v_stored = [sem(f"v_stored{s}") for s in range(2)]
        norm1_ready = sem("norm1_ready")
        xin_in = [sem(f"xin_in{s}") for s in range(2)]
        vc_in = [sem(f"vc_in{s}") for s in range(2)]
        y_done, x1_done, t_done, gx_done = sem("y_done"), sem("x1_done"), sem("t_done"), sem("gx_done")
        u_done, conv_done, r_done, rt_done = sem("u_done"), sem("conv_done"), sem("r_done"), sem("rt_done")
        out_done = sem("out_done")
        stored = [sem(f"stored{s}") for s in range(4)]

        def wait(eng, s, value):
            if not isinstance(value, int) or value > 0:
                eng.wait_ge(s, value)

        XT_USE = 16 * HH
        block = ctx.enter_context(nc.Block())

        @block.sync
        def _(sp):
            sp.dma_start(T[:, :], tab).then_inc(tables_in, 16)

            def load_tiles(b, first):
                for i in range(TILES):
                    if not (first and i < 2):
                        sp.wait_ge(squared, 2 * TILES * b + 2 * (i - 1))
                        sp.wait_ge(z_copied, 2 * TILES * b + 2 * (i - 1))
                    for hh in range(HH):
                        dst = tile[i % 2][:, hh, :].rearrange("p (half n) -> p half n", half=2)
                        src = x_tiles[b, i, hh] if first else x_tiles[bass.ds(b, 1), i, hh, :, :, :][0]
                        sp.dma_start(dst, src).then_inc(tile_in[i % 2], 16)

            load_tiles(0, True)
            with sp.Fori(1, B) as b:
                load_tiles(b, False)

            sp.wait_ge(squared, 2 * B * TILES)
            sp.wait_ge(z_copied, 2 * B * TILES)
            for q in range(4):
                src = spec_w[:, 8 * q:8 * q + 8].rearrange("kx ky c d -> c ky kx d")
                for k in range(8):
                    sp.dma_start(spec[32 * q:32 * q + 32, k * 1024:(k + 1) * 1024]
                                 .rearrange("c (kx d) -> c kx d", d=C), src[:, k]).then_inc(spec_in, 16)
            sp.wait_ge(x_copied, 2 * B)
            sp.dma_start(X_dram.rearrange("b k c m -> k b (c m)"), X[0:64]).then_inc(x_stored, 16)
            sp.wait_ge(x_stored, 16)
            for q in range(4):
                for n in range(8):
                    src = X_dram.rearrange("b (ri q k) c m -> q k c (b ri) m", ri=2, q=4)[q, n]
                    sp.dma_start(XC[32 * q:32 * q + 32, :, 32 * n:32 * n + 32], src).then_inc(xc_in, 16)
            sp.wait_ge(o_copied, 16)
            for q in range(4):
                sp.dma_start(O_dram[:, 8 * q:8 * q + 8].rearrange("r k m d -> r (k m d)"),
                             O_part[32 * q:32 * q + 16, :]).then_inc(o_stored, 16)
            sp.wait_ge(o_stored, 64)
            sp.wait_ge(lv_zero, 1)

            def load_pair(i):
                for s in range(2):
                    b = 2 * i + s
                    src = O_dram[2 * b:2 * b + 2].rearrange("ri ky kx d -> ri kx ky d")
                    for part in range(2):
                        for ri in range(2):
                            rows = 64 * s + 32 * part
                            m = 64 * s + 32 * (ri ^ part)
                            sp.dma_start(LV[i % 2][rows:rows + 32, m:m + 32, :], src[ri]).then_inc(lv_in[i % 2], 16)

            load_pair(0)
            for ri in range(2):
                sp.dma_start(O[32 * ri:32 * ri + 32],
                             O_dram.rearrange("(b ri) ky kx d -> ri ky b (kx d)", ri=2)[ri]).then_inc(o_in, 16)
            load_pair(1)
            for n in range(8):
                i, half = n // 2, n % 2
                sp.wait_ge(v_copied_act, 16 * (n + 1))
                sp.wait_ge(v_copied_dve, 16 * (n + 1))
                for s in range(2):
                    dst = V_dram[VH // CH * half:VH // CH * (half + 1), :, 2 * i + s].rearrange("n k m -> k n m")
                    sp.dma_start(dst, VS[n % 2][64 * s:64 * s + 64].rearrange("k (n h) d -> k n (h d)", h=CH)
                                 ).then_inc(v_stored[n % 2], 16)
                if half and i < 2:
                    load_pair(i + 2)

            def load_chunk(c, c_slot):
                wait(sp, x1_done, 8 * c - 8)
                sp.wait_ge(norm1_ready, 1)
                for b in range(B):
                    sp.dma_start(x_in[c_slot % 2][:, b], x_rows[b, :, bass.ds(CH * c, CH), :]
                                 ).then_inc(xin_in[c_slot % 2], 16)
                for g in range(G):
                    src = V_dram[bass.ds(c, 1), :, BG * g:BG * (g + 1), :][0].rearrange("k b m -> k (b m)")
                    sp.dma_start(Vc[c_slot % 2][64 * g:64 * g + 64, :], src).then_inc(vc_in[c_slot % 2], 16)

            def store_chunk(c, c_slot):
                sp.wait_ge(out_done, 8 * c + 8)
                sp.wait_ge(norm1_ready, 1)
                for b in range(B):
                    sp.dma_start(out_rows[b, :, bass.ds(CH * c, CH), :], x1[c_slot][:, b]
                                 ).then_inc(stored[c_slot], 16)

            for s in range(2):
                sp.wait_ge(v_stored[s], 4 * 32)
            for c in range(4):
                load_chunk(c, c)
            with sp.Fori(0, CHUNKS // 4 - 1) as it:
                for s in range(4):
                    load_chunk(4 * it + (s + 4), s)
                    store_chunk(4 * it + s, s)
            for s in range(4):
                store_chunk(CHUNKS - 4 + s, s)
            for s in range(4):
                sp.wait_ge(stored[s], 128 * (CHUNKS // 4))

        @block.gpsimd
        def _(pool):
            nc.gpsimd.memset(conv[:, :, :], 0.0).then_inc(conv_zero, 1)
            pool.wait_ge(conv_zero, 1)
            n = 0
            for m, (shift, first) in enumerate(((-4, 0), (0, 0), (0, 2), (4, 2))):
                for i in range(4):
                    for o in range(first, first + 2):
                        tap = i + shift - o + 2
                        if 0 <= tap < 5:
                            pool.dma_start(conv[32 * i:32 * i + 32, m, 32 * (o % 2):32 * (o % 2) + 32],
                                           conv_w[:, tap, 0, :]).then_inc(conv_in, 16)
                            n += 1
            assert n == 20
            for i in range(4):
                pool.dma_start(bias[32 * i:32 * i + 32, :], conv_b.rearrange("(c n) -> c n", n=1)).then_inc(bias_in, 16)
            pool.wait_ge(mix_done, 16)
            for s in range(2):
                nc.gpsimd.memset(LV[s][0:64, 64:128, :], 0.0)
                last = nc.gpsimd.memset(LV[s][64:128, 0:64, :], 0.0)
            last.then_inc(lv_zero, 1)

        @block.tensor
        def _(pe):
            pe.wait_ge(tables_in, 16)
            dft_h = table("dft_h").rearrange("p (hh k) -> p hh k", hh=HH)
            dft_w = table("dft_w").rearrange("p (s w k) -> p s w k", s=2, w=4)
            ident = table("ident")

            def forward(b):
                for i in range(TILES):
                    pe.wait_ge(tile_in[i % 2], XT_USE * (TILES // 2 * b + i // 2 + 1))
                    for blk in range(2):
                        n = 2 * TILES * b + 2 * i + blk
                        wait(pe, z_copied, n - 3)
                        for hh in range(HH):
                            for half in range(2):
                                at = half * TW * C + blk * BANK
                                last = nc.tensor.matmul(ps[(2 * i + blk) % 4][64 * half:64 * half + 64, :],
                                                        dft_h[:, hh, :], tile[i % 2][:, hh, at:at + BANK],
                                                        start=(hh == 0), stop=(hh == HH - 1))
                        last.then_inc(rowdft_done, 1)
                pe.wait_ge(z_copied, 2 * TILES * (b + 1))
                for m in range(16):
                    sub, c4 = m // 8, m % 8
                    wait(pe, zt_copied, 16 * b + m - 1)
                    for c in range(4):
                        last = nc.tensor.transpose(ps[4 + m % 2][:, P * c:P * (c + 1)],
                                                   Z[:, 4 * c4 + c, P * sub:P * (sub + 1)], ident)
                    last.then_inc(zt_done, 1)
                pe.wait_ge(zt_copied, 16 * (b + 1))
                for e in range(2):
                    wait(pe, x_copied, 2 * b + e - 1)
                    for k in range(8):
                        half, sub, cs = k // 4, k // 2 % 2, k % 2
                        at = 64 * half + 32 * cs
                        last = nc.tensor.matmul(ps[6 + e][0:64, :], dft_w[:, cs, 2 * half + sub, :],
                                                ZT[sub][:, 16 * e:16 * e + 16, at:at + 32],
                                                start=(k == 0), stop=(k == 7))
                    last.then_inc(coldft_done, 1)

            forward(0)
            with pe.Fori(1, B) as b:
                forward(b)

            pe.wait_ge(sums_ready, 1)
            nc.tensor.matmul(ps[0][:, 0:16 * B], table("ones"), sumsq[:, :], start=True, stop=True)
            nc.tensor.matmul(ps[1][:, 0:C * B], table("dc", 0, 64),
                             X[0:64].rearrange("k b (c m) -> k b c m", m=M)[:, :, :, 0],
                             start=True, stop=True).then_inc(sums_done, 1)

            pe.wait_ge(xc_scaled, 1)
            pe.wait_ge(spec_in, 16 * 32)
            for e in range(16):
                wait(pe, o_copied, e - 1)
                for kx in range(16):
                    for q in range(4):
                        rows = slice(32 * q, 32 * q + 32)
                        at = BANK * e + C * kx
                        last = nc.tensor.matmul(ps[4 * (e % 2) + q][32 * q:32 * q + 16, C * kx:C * (kx + 1)],
                                                XC[rows, :, 16 * e + kx], spec[rows, at:at + C],
                                                start=True, stop=True)
                last.then_inc(mix_done, 1)

            idft_h = table("idft_h")
            n = 0
            for i in range(4):
                pe.wait_ge(lv_signed, i + 1)
                for half in range(2):
                    for d in range(C):
                        wait(pe, v_copied_dve if n % 2 else v_copied_act, n // 2 - 1)
                        nc.tensor.matmul(ps[n % 4][:, 0:VH], LV[i % 2][:, :, d],
                                         idft_h[:, VH * half:VH * (half + 1)],
                                         start=True, stop=True).then_inc(v_done, 1)
                        n += 1

            pe.wait_ge(sums_ready, 2)
            nc.tensor.matmul(ps[4][:, 0:C * B], table("cross", 0, 64), R1[0:64, :], start=True, stop=False)
            nc.tensor.matmul(ps[4][:, 0:C * B], table("power", 0, 64), R2[0:64, :], start=False, stop=False)
            nc.tensor.matmul(ps[4][:, 0:C * B], table("power0", 0, 64), R3[0:64, :], start=False, stop=True)
            nc.tensor.matmul(ps[5][:, 0:C * B], table("dc", 0, 64),
                             O[0:64, :, 0:C], start=True, stop=True).then_inc(sums_done, 1)

            idft_w = table("idft_w").rearrange("p (g q j) -> p g q j", g=G, q=4)

            def column_idft(n, slot, q, g):
                if q == 0 and g == 0:
                    c = n // 4 if isinstance(n, int) else None
                wait(pe, x1_done, 2 * (n - 1) + g + 1)
                nc.tensor.matmul(ps[g][:, :], idft_w[:, g, q, :], Vc[slot % 2][:, :],
                                 start=True, stop=True).then_inc(y_done, 1)

            def transpose_x1(n, slot, q, k):
                wait(pe, gx_done, 2 * (n - 1) + k + 1)
                for h in range(CH):
                    last = nc.tensor.transpose(ps[2 + k][:, P * h:P * (h + 1)], x1[slot][:, 2 * q + k, h, :], ident)
                last.then_inc(t_done, 1)

            def convolve(t, g):
                pe.wait_ge(u_done, 2 * t + g + 1)
                wait(pe, r_done, 2 * (t - 1) + g + 1)
                bank = ps[4 + g]
                for m, shift in ((0, 0), (2, 1), (1, 1), (3, 2)):
                    half = m // 2
                    last = nc.tensor.matmul(bank[64 * half:64 * half + 64, :], conv[:, m, :],
                                            u[g][:, :, shift:shift + P], start=(m % 2 == 0) if half == 0 else (m == 2),
                                            stop=(m % 2 == 1))
                last.then_inc(conv_done, 1)

            def transpose_r(t, t_slot, g):
                pe.wait_ge(r_done, 2 * t + g + 1)
                wait(pe, out_done, 2 * (t - 1) + g + 1)
                for b in range(BG):
                    last = nc.tensor.transpose(ps[6 + g][:, P * b:P * (b + 1)],
                                               r[g][t_slot % 2][:, P * b:P * (b + 1)], ident)
                last.then_inc(rt_done, 1)

            def prep_y(n, s, base, gs):
                slot, q = s // 4, s % 4
                for g in gs:
                    if q == 0 and g == 0:
                        pe.wait_ge(vc_in[slot % 2], 32 * ((base // 4 + slot) // 2 + 1) if isinstance(base, int)
                                   else 32 * (slot // 2 + 1) + base * 4)
                    column_idft(n, slot, q, g)

            def prep_t(n, s, base):
                slot, q = s // 4, s % 4
                if q == 0:
                    pe.wait_ge(x1_done, 2 * n + 8)
                for k in range(2):
                    transpose_x1(n, slot % 4, q, k)

            for n in range(9):
                prep_y(n, n, 0, (0, 1))
            for n in range(5):
                prep_t(n, n, 0)

            def steps(base):
                for s in range(STEPS):
                    t = base + s
                    last_y = isinstance(base, int) and t + 9 >= H
                    last_t = isinstance(base, int) and t + 5 >= H
                    convolve(t, 0)
                    if not (isinstance(base, int) and t == 0):
                        transpose_r(t - 1, s - 1, 1)
                    if not last_y:
                        prep_y(t + 9, s + 9, base, (0,))
                    convolve(t, 1)
                    transpose_r(t, s, 0)
                    if not last_y:
                        prep_y(t + 9, s + 9, base, (1,))
                    if not last_t:
                        prep_t(t + 5, s + 5, base)

            pe.wait_ge(conv_in, 16 * 20)
            steps(0)
            with pe.Fori(1, H // STEPS - 1) as it:
                steps(STEPS * it)
            steps(H - STEPS)
            transpose_r(H - 1, STEPS - 1, 1)

        @block.scalar
        def _(act):
            def squares(b):
                for i in range(TILES):
                    act.wait_ge(tile_in[i % 2], XT_USE * (TILES // 2 * b + i // 2 + 1))
                    flat = tile[i % 2].rearrange("p hh (w c) -> p (hh w) c", c=C)
                    for g in range(SQ_ACT):
                        at = (b * TILES + i) * 16 + g
                        if g == 1:
                            wait(act, squared, 2 * (b * TILES + i))
                        else:
                            wait(act, sq_act, (SQ_ACT - 1) * (b * TILES + i) + max(g - 1, 0))
                        ins = nc.scalar.activation(squares_act[g % 2], flat[:, :, 2 * g:2 * g + 2], ACT.Square,
                                                   accum_out=sq[:, bass.ds(at, 1)])
                        if g < SQ_ACT - 1:
                            ins.then_inc(sq_act, 1)
                        else:
                            ins.then_inc(squared, 2)

            squares(0)
            with act.Fori(1, B) as b:
                squares(b)

            act.wait_ge(var_ready, 1)
            nc.scalar.activation(small[:, 3, :], small[:, 2, :], ACT.Sqrt).then_inc(root_done, 1)

            def evac(s, e):
                act.wait_ge(mix_done, e + s + 1)
                for q in range(4):
                    dst = O_part[32 * q:32 * q + 16, bass.ds(BANK * (e + s), BANK)]
                    last = nc.scalar.activation(dst, ps[4 * s + q][32 * q:32 * q + 16, :], ACT.Copy)
                last.then_inc(o_copied, 1)

            with act.Fori(0, 8) as it:
                for s in range(2):
                    evac(s, 2 * it)

            for n in range(8):
                if n >= 2:
                    act.wait_ge(v_stored[n % 2], 32 * (n // 2))
                for d in range(0, C, 2):
                    act.wait_ge(v_done, C * n + d + 1)
                    nc.scalar.activation(VS[n % 2][:, :, d], ps[d % 4][:, 0:VH], ACT.Copy).then_inc(v_copied_act, 1)

            act.wait_ge(var_ready, 2)
            nc.scalar.activation(small[:, 9, :], small[:, 8, :], ACT.Sqrt).then_inc(root_done, 1)

            def relu(t, t_slot, g):
                if isinstance(t, int) and t == H - 1:
                    act.wait_ge(conv_done, 2 * t + g + 1)
                else:
                    act.wait_ge(u_done, 2 * t + g + 3)
                wait(act, rt_done, 2 * (t - 2) + g + 1)
                nc.scalar.activation(r[g][t_slot % 2], ps[4 + g][:, :], ACT.Relu, bias=bias[:, 0:1]).then_inc(r_done, 1)

            def normalise(n, s):
                slot, q = s // 4, s % 4
                if q == 0:
                    wait(act, u_done, 2 * n - 8)
                for k in range(2):
                    b = 2 * q + k
                    act.wait_ge(t_done, 2 * n + k + 1)
                    nc.scalar.activation(gx[slot % 2][:, b], ps[2 + k][:, :].rearrange("p (h j) -> p h j", h=CH),
                                         ACT.Identity, scale=small[:, 11, b:b + 1],
                                         bias=small[:, 13, b:b + 1]).then_inc(gx_done, 1)

            act.wait_ge(norm1_ready, 1)
            act.wait_ge(bias_in, 64)
            for n in range(5):
                normalise(n, n)

            def steps(base):
                for s in range(STEPS):
                    t = base + s
                    relu(t, s, 0)
                    relu(t, s, 1)
                    if not (isinstance(base, int) and t + 5 >= H):
                        normalise(t + 5, s + 5)

            steps(0)
            with act.Fori(1, H // STEPS - 1) as it:
                steps(STEPS * it)
            steps(H - STEPS)

        @block.vector
        def _(dve):
            chain = [0]

            def link(ins):
                chain[0] += 1
                ins.then_inc(dve_step, 1)
                dve.wait_ge(dve_step, chain[0])

            dve.wait_ge(tables_in, 16)

            def forward(b):
                for i in range(TILES):
                    dve.wait_ge(tile_in[i % 2], XT_USE * (TILES // 2 * b + i // 2 + 1))
                    flat = tile[i % 2].rearrange("p hh (w c) -> p (hh w) c", c=C)
                    for g in range(SQ_ACT, 16):
                        at = (b * TILES + i) * 16 + g
                        v = flat[:, :, 2 * g:2 * g + 2]
                        n = (b * TILES + i) * SQ_DVE + g - SQ_ACT
                        wait(dve, sq_dve, n - 1)
                        nc.vector.scalar_tensor_tensor(squares_dve[g % 2], v, 1.0, v, ALU.mult, ALU.mult,
                                                       accum_out=sq[:, bass.ds(at, 1)]).then_inc(sq_dve, 1)
                    for blk in range(2):
                        dve.wait_ge(rowdft_done, 2 * TILES * b + 2 * i + blk + 1)
                        at = i * TW + 16 * blk
                        nc.vector.tensor_copy(Z[:, :, at:at + 16],
                                              ps[(2 * i + blk) % 4][:, :].rearrange("p (w c) -> p c w", c=C)
                                              ).then_inc(z_copied, 1)
                for m in range(16):
                    dve.wait_ge(zt_done, 16 * b + m + 1)
                    c = 4 * (m % 8)
                    nc.vector.tensor_copy(ZT[m // 8][:, c:c + 4, :],
                                          ps[4 + m % 2][:, :].rearrange("p (c k) -> p c k", c=4)).then_inc(zt_copied, 1)
                for e in range(2):
                    dve.wait_ge(coldft_done, 2 * b + e + 1)
                    dst = X[0:64, b, BANK * e:BANK * (e + 1)] if isinstance(b, int) else \
                        X[0:64, bass.ds(b, 1), BANK * e:BANK * (e + 1)].rearrange("p b n -> p (b n)")
                    nc.vector.tensor_copy(dst, ps[6 + e][0:64, :]).then_inc(x_copied, 1)

            forward(0)
            with dve.Fori(1, B) as b:
                forward(b)

            dve.wait_ge(bias_in, 64)
            link(nc.vector.tensor_scalar(neg_bias[:, :], bias[:, :], -1.0, None, ALU.mult))
            dve.wait_ge(squared, 2 * B * TILES)
            dve.wait_ge(sq_act, (SQ_ACT - 1) * B * TILES)
            dve.wait_ge(sq_dve, SQ_DVE * B * TILES)
            nc.vector.tensor_reduce(sumsq[:, :].rearrange("p (b g) -> p b g", b=B),
                                    sq[:, :].rearrange("p (b t g) -> p b g t", b=B, g=16),
                                    AX.X, ALU.add).then_inc(sums_ready, 1)
            dve.wait_ge(sums_done, 1)

            def group_sum(dst, bank, n, mask):
                v = masked[:, 0:B * n].rearrange("p (b g) -> p b g", b=B)
                m = table(mask).rearrange("p (b g) -> p b g", b=1).broadcast_to([P, B, n])
                link(nc.vector.tensor_tensor(v, bank[:, 0:B * n].rearrange("p (b g) -> p b g", b=B), m, ALU.mult))
                link(nc.vector.tensor_reduce(dst, v, AX.X, ALU.add))

            def variance(total, total_sq, mean, var, tmp):
                link(nc.vector.tensor_scalar(mean, total, 1.0 / N2, None, ALU.mult))
                link(nc.vector.tensor_tensor(tmp, mean, mean, ALU.mult))
                link(nc.vector.scalar_tensor_tensor(var, total_sq, 1.0 / N2, tmp, ALU.mult, ALU.subtract))
                nc.vector.tensor_scalar(var, var, 0.0, GN_EPS, ALU.max, ALU.add).then_inc(var_ready, 1)

            def reciprocal_root(var, root, tmp, dst):
                link(nc.vector.reciprocal(tmp, root))
                link(nc.vector.tensor_tensor(tmp, tmp, var, ALU.mult))
                link(nc.vector.tensor_tensor(tmp, tmp, root, ALU.add))
                link(nc.vector.tensor_scalar(tmp, tmp, 0.5, None, ALU.mult))
                link(nc.vector.reciprocal(dst, tmp))

            group_sum(small[:, 0, :], ps[0], 16, "same_group16")
            group_sum(small[:, 1, :], ps[1], 32, "same_group32")
            variance(small[:, 1, :], small[:, 0, :], small[:, 5, :], small[:, 2, :], small[:, 4, :])
            dve.wait_ge(root_done, 1)
            reciprocal_root(small[:, 2, :], small[:, 3, :], small[:, 4, :], small[:, 6, :])
            dve.wait_ge(xc_in, 16 * 32)
            zero_mode = XC[0:32, :, 0].rearrange("p (b ri) -> p b ri", ri=2)[:, :, 0]
            link(nc.vector.scalar_tensor_tensor(zero_mode, small[0:32, 1, :], -0.5, zero_mode, ALU.mult, ALU.add))
            for b in range(B):
                ins = nc.vector.tensor_scalar(XC[:, 2 * b:2 * b + 2, :], XC[:, 2 * b:2 * b + 2, :],
                                              small[:, 6, b:b + 1], None, ALU.mult)
            ins.then_inc(xc_scaled, 1)

            for i in range(4):
                dve.wait_ge(lv_in[i % 2], 128 * (i // 2 + 1))
                for s in range(2):
                    v = LV[i % 2][64 * s + 32:64 * s + 64, 64 * s:64 * s + 32, :]
                    ins = nc.vector.tensor_scalar(v, v, -1.0, None, ALU.mult)
                ins.then_inc(lv_signed, 1)
                if i == 0:
                    dve.wait_ge(o_in, 32)
                for half in range(2):
                    m = 2 * i + half
                    if m >= 2:
                        dve.wait_ge(v_stored[m % 2], 32 * (m // 2))
                    for d in range(1, C, 2):
                        dve.wait_ge(v_done, C * m + d + 1)
                        nc.vector.tensor_copy(VS[m % 2][:, :, d], ps[d % 4][:, 0:VH]).then_inc(v_copied_dve, 1)
                    b = m
                    pr = prod[0:64, 0:C * M].rearrange("p (c m) -> p c m", m=M)
                    o_t = O[0:64, b].rearrange("p (m c) -> p c m", c=C)
                    link(nc.vector.tensor_tensor(pr, X[0:64, b].rearrange("p (c m) -> p c m", m=M), o_t, ALU.mult))
                    link(nc.vector.tensor_reduce(R1[0:64, C * b:C * (b + 1)], pr, AX.X, ALU.add))
                    link(nc.vector.tensor_tensor(pr, o_t, o_t, ALU.mult))
                    nc.vector.tensor_copy(R3[0:64, C * b:C * (b + 1)], pr[:, :, 0])
                    ins = nc.vector.tensor_reduce(R2[0:64, C * b:C * (b + 1)], pr, AX.X, ALU.add)
                    if b < B - 1:
                        link(ins)
            ins.then_inc(sums_ready, 1)
            dve.wait_ge(sums_done, 2)
            group_sum(small[:, 7, :], ps[4], 32, "same_group32")
            link(nc.vector.tensor_tensor(small[:, 7, :], small[:, 7, :], small[:, 0, :], ALU.add))
            group_sum(small[:, 10, :], ps[5], 32, "same_group32")
            link(nc.vector.tensor_tensor(small[:, 10, :], small[:, 10, :], small[:, 1, :], ALU.add))
            variance(small[:, 10, :], small[:, 7, :], small[:, 12, :], small[:, 8, :], small[:, 4, :])
            dve.wait_ge(root_done, 2)
            reciprocal_root(small[:, 8, :], small[:, 9, :], small[:, 4, :], small[:, 11, :])
            link(nc.vector.tensor_tensor(small[:, 13, :], small[:, 12, :], small[:, 11, :], ALU.mult))
            link(nc.vector.tensor_scalar(small[:, 13, :], small[:, 13, :], -1.0, bias[:, 0:1], ALU.mult, ALU.add))
            for g in range(G):
                nc.vector.memset(u[g][:, :, 0:1], 0.0)
                ins = nc.vector.memset(u[g][:, :, 129:130], 0.0)
            ins.then_inc(norm1_ready, 1)

            def add_y(n, s, base, g):
                slot, q = s // 4, s % 4
                if q == 0 and g == 0:
                    if isinstance(base, int):
                        c = base // 4 + slot
                        dve.wait_ge(xin_in[slot % 2], 128 * (c // 2 + 1))
                        wait(dve, stored[slot % 4], 128 * (c // 4))
                    else:
                        dve.wait_ge(xin_in[slot % 2], 128 * (slot // 2 + 1) + base * 16)
                        dve.wait_ge(stored[slot % 4], 128 * (slot // 4) + base * 8)
                dve.wait_ge(y_done, 2 * n + g + 1)
                src = x_in[slot % 2][:, BG * g:BG * (g + 1), :, C * q:C * (q + 1)]
                dst = x1[slot % 4][:, BG * g:BG * (g + 1), :, C * q:C * (q + 1)]
                y = ps[g][:, :].rearrange("p (b h c) -> p b h c", b=BG, h=CH)
                nc.vector.tensor_tensor(dst, y, src, ALU.add).then_inc(x1_done, 1)

            def next_u(t, s, base, g):
                slot, row = (s + 1) // 4, (s + 1) % 4
                dve.wait_ge(conv_done, 2 * t + g + 1)
                if row == 0:
                    dve.wait_ge(gx_done, 2 * (t + 1) + 4 * g + 4)
                nc.vector.scalar_tensor_tensor(
                    u[g][:, :, 1:129], ps[4 + g][:, :].rearrange("p (b j) -> p b j", b=BG), neg_bias[:, 0:1],
                    gx[slot % 2][:, BG * g:BG * (g + 1), row, :], ALU.max, ALU.add).then_inc(u_done, 1)

            def add_r(t, s, g):
                dve.wait_ge(rt_done, 2 * t + g + 1)
                v = x1[s // 4 % 4][:, BG * g:BG * (g + 1), s % 4, :]
                nc.vector.tensor_tensor(v, ps[6 + g][:, :].rearrange("p (b n) -> p b n", b=BG), v,
                                        ALU.add).then_inc(out_done, 1)

            for n in range(9):
                for g in range(G):
                    add_y(n, n, 0, g)
            for g in range(G):
                dve.wait_ge(gx_done, 4 * g + 4)
                nc.vector.tensor_scalar(u[g][:, :, 1:129], gx[0][:, BG * g:BG * (g + 1), 0, :],
                                        bias[:, 0:1], None, ALU.subtract).then_inc(u_done, 1)

            def steps(base):
                known = isinstance(base, int)
                for s in range(STEPS):
                    t = base + s
                    for g in range(G):
                        if not (known and t + 1 >= H):
                            next_u(t, s, base, g)
                        if g == 1:
                            add_r(t, s, 0)
                        elif not (known and t == 0):
                            add_r(t - 1, s + STEPS - 1, 1)
                        if not (known and t + 9 >= H):
                            add_y(t + 9, s + 9, base, g)

            steps(0)
            with dve.Fori(1, H // STEPS - 1) as it:
                steps(STEPS * it)
            steps(H - STEPS)
            add_r(H - 1, STEPS - 1, 1)


_INS = ["x", "L0_conv_W", "L1_conv_w", "L1_conv_b"]


def kernel(**inputs):
    import numpy as _np
    import concourse.bacc as _bacc
    from concourse import mybir as _mybir
    from concourse.bass_utils import run_bass_kernel_spmd as _run

    nc = _bacc.Bacc("TRN2", target_bir_lowering=False, num_devices=1)
    shape = inputs["x"].shape
    arrays, args = {}, []
    named = [(name, _np.ascontiguousarray(inputs[name])) for name in _INS]
    for name, a in named + [("tables", tables(shape[1], shape[2]))]:
        arrays[f"in_{name}_dram"] = a
        args.append(nc.dram_tensor(f"in_{name}_dram", a.shape, _mybir.dt.from_np(a.dtype), kind="ExternalInput").ap())
    args.append(nc.dram_tensor("out_0_dram", shape, _mybir.dt.float32, kind="ExternalOutput").ap())
    conv_preact_pair(nc, *args)
    r = _run(nc, [arrays], core_ids=[0])
    return r.results[0]["out_0_dram"]
```

```python
from contextlib import ExitStack

import concourse.bass as bass
import numpy as np
from concourse import mybir

F32 = mybir.dt.float32
F32R = mybir.dt.float32r
ALU = mybir.AluOpType
ACT = mybir.ActivationFunctionType
AX = mybir.AxisListType

P = 128
BANK = 512
M = 32
GN_EPS = 1e-5


def table_layout(H):
    sizes = [("dft_h", H // P * 64), ("dft_w", 2 * 4 * 64), ("idft_h", H), ("idft_w", 4 * P),
             ("ident", P), ("ones", P), ("dc", P), ("cross", P), ("power", P), ("power0", P),
             ("same_group16", 16), ("same_group32", 32)]
    at, cols = 0, {}
    for name, n in sizes:
        cols[name] = (at, n)
        at += n
    return cols, at


def tables(H, W):
    cols, total = table_layout(H)
    out = np.zeros((P, total))

    def put(name, rows, values):
        at, n = cols[name]
        out[rows, at:at + n] = values.reshape(values.shape[0], n)

    every = slice(0, P)
    p, k = np.arange(P), np.arange(M)
    h = (np.arange(H // P)[None, :] * P + p[:, None])[:, :, None] * k * (2 * np.pi / H)
    put("dft_h", every, np.concatenate([np.cos(h), np.sin(h)], -1))
    w = (np.arange(4)[None, :] * P + p[:, None])[:, :, None] * k * (2 * np.pi / W)
    put("dft_w", every, np.stack([np.concatenate([np.cos(w), -np.sin(w)], -1),
                                  np.concatenate([-np.sin(w), -np.cos(w)], -1)], 1))
    a = k[:, None] * np.arange(H) * (2 * np.pi / H)
    put("idft_h", every, np.concatenate([np.cos(a), np.sin(a)] * 2, 0))
    N = H * W
    twice = np.where(k == 0, 1.0, 2.0)
    pos = 4 * np.arange(P)[None, :] + np.arange(4)[:, None]
    a = k[:, None, None] * pos * (2 * np.pi / W)
    t = twice[:, None, None] / N * np.stack([np.cos(a), -np.sin(a)])
    t = t.reshape(64, 4 * P)
    put("idft_w", every, np.concatenate([t, t], 0))
    put("ident", every, np.eye(P))
    put("ones", every, np.ones((P, P)))
    rows = slice(0, 64)
    wide = np.ones((1, P))
    dc = np.zeros((64, 1))
    dc[0] = 1
    put("dc", rows, dc * wide)
    put("cross", rows, np.tile(2 * twice / N, 2)[:, None] * wide)
    put("power", rows, np.tile(np.where(k == 0, 0.5, 2.0) / N, 2)[:, None] * wide)
    p0 = np.zeros((64, 1))
    p0[0], p0[M] = 0.5 / N, -0.5 / N
    put("power0", rows, p0 * wide)
    group = (p % 32) // 2
    put("same_group16", every, (group[:, None] == np.arange(16)).astype(float))
    put("same_group32", every, (group[:, None] == np.arange(32) // 2).astype(float))
    return out.astype(np.float32)


def conv_preact_pair(nc, x, spec_w, conv_w, conv_b, tab, out):
    B, H, W, C = x.shape
    assert (B, W, C) == (8, 512, 32) and H % P == 0
    HH = H // P
    G = 2
    BG = B // G
    ROW = W * C
    TW = 32
    TILES = W // 2 // TW
    TILE = 2 * TW * C
    SQ_ACT = 10
    SQ_DVE = 16 - SQ_ACT
    CH = 4
    CHUNKS = H // CH
    STEPS = 16
    N2 = float(2 * H * W)

    x_tiles = x.rearrange("b (hh p) (half i w) c -> b i hh p half (w c)", p=P, half=2, i=TILES)
    x_rows = x.rearrange("b h (j q) c -> b j h (q c)", q=4)
    out_rows = out.rearrange("b h (j q) c -> b j h (q c)", q=4)
    X_dram = nc.dram_tensor("modes_in", (B, 64, C, M), F32, kind="Internal").ap()
    O_dram = nc.dram_tensor("modes_out", (2 * B, M, M, C), F32, kind="Internal").ap()
    V_dram = nc.dram_tensor("row_spectra", (CHUNKS, 64, B, CH * C), F32, kind="Internal").ap()

    ctx = ExitStack()
    with ctx:
        def sb(name, cols):
            return ctx.enter_context(nc.sbuf_tensor(name, [P, cols], F32))

        def sem(name):
            return ctx.enter_context(nc.semaphore(name))

        cols, total = table_layout(H)
        T = sb("tables", total)

        def table(name, lo=0, hi=P):
            at, n = cols[name]
            return T[lo:hi, at:at + n]

        KB = 256
        arena = sb("arena", 164 * KB)

        def region(kb, size_kb):
            return arena[:, kb * KB:(kb + size_kb) * KB]

        tile = [region(32 * s, 8 * HH).rearrange("p (hh n) -> p hh n", hh=HH) for s in range(2)]
        Z = region(64, 32).rearrange("p (c w) -> p c w", c=C)
        ZT = region(96, 16).rearrange("p (c k) -> p c k", c=C)
        X = region(128, 32).rearrange("p (b n) -> p b n", b=B)
        sq = sb("sq", B * TILES * 16)
        SQ = TILE * HH // 16
        squares_act = [region(160 + 2 * s, 2)[:, 0:SQ].rearrange("p (w c) -> p w c", c=2) for s in range(2)]
        squares_dve = [sb(f"squares_dve{s}", SQ).rearrange("p (w c) -> p w c", c=2) for s in range(2)]
        spec = region(0, 32)
        O_part = region(32, 32)
        XC = region(64, 16).rearrange("p (r n) -> p r n", r=2 * B)
        O = region(96, 32).rearrange("p (b n) -> p b n", b=B)
        LV = [region(16 * s, 16).rearrange("p (m d) -> p m d", d=C) for s in range(2)]
        VH = H // 2
        VS = [region(32 + 32 * s, H // 16).rearrange("p (h d) -> p h d", d=C) for s in range(2)]
        prod = region(160, 4)
        x_in = [region(16 * s, 16).rearrange("p (b h n) -> p b h n", b=B, h=CH) for s in range(2)]
        x1 = [region(32 + 16 * s, 16).rearrange("p (b h n) -> p b h n", b=B, h=CH) for s in range(4)]
        gx = [region(96 + 16 * s, 16).rearrange("p (b h n) -> p b h n", b=B, h=CH) for s in range(2)]
        Vc = [region(128 + 4 * s, 4) for s in range(2)]
        r = [[region(136 + 4 * g + 2 * s, 2) for s in range(2)] for g in range(G)]
        u = [arena[:, 144 * KB + g * BG * 130:144 * KB + (g + 1) * BG * 130]
             .rearrange("p (b j) -> p b j", b=BG) for g in range(G)]
        V_parts = [ctx.enter_context(nc.sbuf_tensor(f"V_parts{s}", [P, G * BANK], F32R)) for s in range(2)]
        W_parts = [ctx.enter_context(nc.sbuf_tensor(f"W_parts{s}", [P, 4 * P], F32R)) for s in range(2)]
        conv = sb("conv_w", 4 * 64).rearrange("p (m n) -> p m n", m=4)
        bias, neg_bias = sb("bias", 1), sb("neg_bias", 1)
        small = sb("small", 16 * B).rearrange("p (n b) -> p n b", b=B)
        sumsq = sb("sumsq", 16 * B)
        masked = sb("masked", C * B)
        R1, R2, R3 = sb("R1", C * B), sb("R2", C * B), sb("R3", C * B)
        ps = [ctx.enter_context(nc.psum_tensor(f"ps{i}", [P, BANK], F32)) for i in range(8)]

        tables_in, bias_in, conv_in = sem("tables_in"), sem("bias_in"), sem("conv_in")
        conv_zero, spec_in = sem("conv_zero"), sem("spec_in")
        tile_in = [sem(f"tile_in{s}") for s in range(2)]
        sq_act, sq_dve, squared = sem("sq_act"), sem("sq_dve"), sem("squared")
        rowdft_done, z_copied = sem("rowdft_done"), sem("z_copied")
        zt_done, zt_copied = sem("zt_done"), sem("zt_copied")
        coldft_done, x_copied, x_stored = sem("coldft_done"), sem("x_copied"), sem("x_stored")
        xc_in, xc_scaled = sem("xc_in"), sem("xc_scaled")
        dve_step, sums_ready, sums_done = sem("dve_step"), sem("sums_ready"), sem("sums_done")
        var_ready, root_done = sem("var_ready"), sem("root_done")
        mix_done, o_copied, o_stored = sem("mix_done"), sem("o_copied"), sem("o_stored")
        o_in, lv_zero, lv_signed = sem("o_in"), sem("lv_zero"), sem("lv_signed")
        lv_in = [sem(f"lv_in{s}") for s in range(2)]
        v_done, v_copied_act, v_copied_dve = sem("v_done"), sem("v_copied_act"), sem("v_copied_dve")
        v_stored = [sem(f"v_stored{s}") for s in range(2)]
        norm1_ready = sem("norm1_ready")
        xin_in = [sem(f"xin_in{s}") for s in range(2)]
        vc_in = [sem(f"vc_in{s}") for s in range(2)]
        w_high, w_low, v_high, v_low = sem("w_high"), sem("w_low"), sem("v_high"), sem("v_low")
        y_done, x1_done, t_done, gx_done = sem("y_done"), sem("x1_done"), sem("t_done"), sem("gx_done")
        u_done, conv_done, r_done, rt_done = sem("u_done"), sem("conv_done"), sem("r_done"), sem("rt_done")
        out_done = sem("out_done")
        stored = [sem(f"stored{s}") for s in range(4)]

        def wait(eng, s, value):
            if not isinstance(value, int) or value > 0:
                eng.wait_ge(s, value)

        XT_USE = 16 * HH

        block = ctx.enter_context(nc.Block())

        @block.sync
        def _(sp):
            sp.dma_start(T[:, :], tab).then_inc(tables_in, 16)

            def load_tiles(b, first):
                for i in range(TILES):
                    if not (first and i < 2):
                        sp.wait_ge(squared, 2 * TILES * b + 2 * (i - 1))
                        sp.wait_ge(z_copied, 2 * TILES * b + 2 * (i - 1))
                    for hh in range(HH):
                        dst = tile[i % 2][:, hh, :].rearrange("p (half n) -> p half n", half=2)
                        src = x_tiles[b, i, hh] if first else x_tiles[bass.ds(b, 1), i, hh, :, :, :][0]
                        sp.dma_start(dst, src).then_inc(tile_in[i % 2], 16)

            load_tiles(0, True)
            with sp.Fori(1, B) as b:
                load_tiles(b, False)

            sp.wait_ge(squared, 2 * B * TILES)
            sp.wait_ge(z_copied, 2 * B * TILES)
            for q in range(4):
                src = spec_w[:, 8 * q:8 * q + 8].rearrange("kx ky c d -> c ky kx d")
                for k in range(8):
                    sp.dma_start(spec[32 * q:32 * q + 32, k * 1024:(k + 1) * 1024]
                                 .rearrange("c (kx d) -> c kx d", d=C), src[:, k]).then_inc(spec_in, 16)
            sp.wait_ge(x_copied, 2 * B)
            sp.dma_start(X_dram.rearrange("b k c m -> k b (c m)"), X[0:64]).then_inc(x_stored, 16)
            sp.wait_ge(x_stored, 16)
            for q in range(4):
                for n in range(8):
                    src = X_dram.rearrange("b (ri q k) c m -> q k c (b ri) m", ri=2, q=4)[q, n]
                    sp.dma_start(XC[32 * q:32 * q + 32, :, 32 * n:32 * n + 32], src).then_inc(xc_in, 16)
            sp.wait_ge(o_copied, 16)
            for q in range(4):
                sp.dma_start(O_dram[:, 8 * q:8 * q + 8].rearrange("r k m d -> r (k m d)"),
                             O_part[32 * q:32 * q + 16, :]).then_inc(o_stored, 16)
            sp.wait_ge(o_stored, 64)
            sp.wait_ge(lv_zero, 1)

            def load_pair(i):
                for s in range(2):
                    b = 2 * i + s
                    src = O_dram[2 * b:2 * b + 2].rearrange("ri ky kx d -> ri kx ky d")
                    for part in range(2):
                        for ri in range(2):
                            rows = 64 * s + 32 * part
                            m = 64 * s + 32 * (ri ^ part)
                            sp.dma_start(LV[i % 2][rows:rows + 32, m:m + 32, :], src[ri]).then_inc(lv_in[i % 2], 16)

            load_pair(0)
            for ri in range(2):
                sp.dma_start(O[32 * ri:32 * ri + 32],
                             O_dram.rearrange("(b ri) ky kx d -> ri ky b (kx d)", ri=2)[ri]).then_inc(o_in, 16)
            load_pair(1)
            for n in range(8):
                i, half = n // 2, n % 2
                sp.wait_ge(v_copied_act, 16 * (n + 1))
                sp.wait_ge(v_copied_dve, 16 * (n + 1))
                for s in range(2):
                    dst = V_dram[VH // CH * half:VH // CH * (half + 1), :, 2 * i + s].rearrange("n k m -> k n m")
                    sp.dma_start(dst, VS[n % 2][64 * s:64 * s + 64].rearrange("k (n h) d -> k n (h d)", h=CH)
                                 ).then_inc(v_stored[n % 2], 16)
                if half and i < 2:
                    load_pair(i + 2)

            def load_spectra(c, slot):
                wait(sp, v_low, c - 1)
                sp.wait_ge(norm1_ready, 1)
                for part in range(2):
                    src = V_dram[bass.ds(c, 1)][0].rearrange("k b m -> k (b m)")
                    sp.dma_start(Vc[slot % 2][64 * part:64 * part + 64, :], src).then_inc(vc_in[slot % 2], 16)

            def load_rows(c, slot):
                wait(sp, x1_done, 8 * c - 8)
                sp.wait_ge(norm1_ready, 1)
                for b in range(B):
                    sp.dma_start(x_in[slot % 2][:, b], x_rows[b, :, bass.ds(CH * c, CH), :]
                                 ).then_inc(xin_in[slot % 2], 16)

            def store_chunk(c, c_slot):
                sp.wait_ge(out_done, 8 * c + 8)
                sp.wait_ge(norm1_ready, 1)
                for b in range(B):
                    sp.dma_start(out_rows[b, :, bass.ds(CH * c, CH), :], x1[c_slot][:, b]
                                 ).then_inc(stored[c_slot], 16)

            for s in range(2):
                sp.wait_ge(v_stored[s], 4 * 32)
            load_spectra(0, 0)
            for c in range(4):
                load_spectra(c + 1, c + 1)
                load_rows(c, c)
            with sp.Fori(0, CHUNKS // 4 - 2) as it:
                for s in range(4):
                    load_spectra(4 * it + (s + 5), s + 1)
                    load_rows(4 * it + (s + 4), s)
                    store_chunk(4 * it + s, s)
            for c in range(CHUNKS - 8, CHUNKS - 4):
                if c + 5 < CHUNKS:
                    load_spectra(c + 5, c + 5)
                load_rows(c + 4, c)
                store_chunk(c, c % 4)
            for s in range(4):
                store_chunk(CHUNKS - 4 + s, s)
            for s in range(4):
                sp.wait_ge(stored[s], 128 * (CHUNKS // 4))

        @block.gpsimd
        def _(pool):
            nc.gpsimd.memset(conv[:, :, :], 0.0).then_inc(conv_zero, 1)
            pool.wait_ge(conv_zero, 1)
            n = 0
            for m, (shift, first) in enumerate(((-4, 0), (0, 0), (0, 2), (4, 2))):
                for i in range(4):
                    for o in range(first, first + 2):
                        tap = i + shift - o + 2
                        if 0 <= tap < 5:
                            pool.dma_start(conv[32 * i:32 * i + 32, m, 32 * (o % 2):32 * (o % 2) + 32],
                                           conv_w[:, tap, 0, :]).then_inc(conv_in, 16)
                            n += 1
            assert n == 20
            for i in range(4):
                pool.dma_start(bias[32 * i:32 * i + 32, :], conv_b.rearrange("(c n) -> c n", n=1)).then_inc(bias_in, 16)
            pool.wait_ge(mix_done, 16)
            for s in range(2):
                nc.gpsimd.memset(LV[s][0:64, 64:128, :], 0.0)
                last = nc.gpsimd.memset(LV[s][64:128, 0:64, :], 0.0)
            last.then_inc(lv_zero, 1)

        @block.tensor
        def _(pe):
            pe.wait_ge(tables_in, 16)
            dft_h = table("dft_h").rearrange("p (hh k) -> p hh k", hh=HH)
            dft_w = table("dft_w").rearrange("p (s w k) -> p s w k", s=2, w=4)
            ident = table("ident")

            def row_dft(b, i):
                pe.wait_ge(tile_in[i % 2], XT_USE * (TILES // 2 * b + i // 2 + 1))
                for blk in range(2):
                    n = 2 * TILES * b + 2 * i + blk
                    wait(pe, z_copied, n - 3)
                    for hh in range(HH):
                        for half in range(2):
                            at = half * TW * C + blk * BANK
                            last = nc.tensor.matmul(ps[(2 * i + blk) % 4][64 * half:64 * half + 64, :],
                                                    dft_h[:, hh, :], tile[i % 2][:, hh, at:at + BANK],
                                                    start=(hh == 0), stop=(hh == HH - 1))
                    last.then_inc(rowdft_done, 1)

            def transpose_z(b, sub, m):
                if m == 0:
                    pe.wait_ge(z_copied, 16 * b + 8 * sub + 8)
                wait(pe, zt_copied, 16 * b + 8 * sub + m - 1)
                for c in range(4):
                    last = nc.tensor.transpose(ps[4 + m % 2][:, P * c:P * (c + 1)],
                                               Z[:, 4 * m + c, P * sub:P * (sub + 1)], ident)
                last.then_inc(zt_done, 1)

            def column_dft(b, sub, e):
                pe.wait_ge(zt_copied, 16 * b + 8 * sub + 4 * e + 4)
                if sub == 0:
                    wait(pe, x_copied, 2 * b + e - 1)
                for k in range(4):
                    half, cs = k // 2, k % 2
                    at = 64 * half + 32 * cs
                    last = nc.tensor.matmul(ps[6 + e][0:64, :], dft_w[:, cs, 2 * half + sub, :],
                                            ZT[:, 16 * e:16 * e + 16, at:at + 32],
                                            start=(sub == 0 and k == 0), stop=(sub == 1 and k == 3))
                last.then_inc(coldft_done, 1)

            def behind(b, i, first):
                if first and i < 4:
                    return
                if i == 0:
                    column_dft(b - 1, 0, 1)
                if i == 4 and not first:
                    column_dft(b - 1, 1, 1)
                prev, sub = (b - 1, 1) if i < 4 else (b, 0)
                for m in (2 * (i % 4), 2 * (i % 4) + 1):
                    transpose_z(prev, sub, m)
                if i % 4 == 2:
                    column_dft(prev, sub, 0)

            def forward(b, first):
                for i in range(TILES):
                    row_dft(b, i)
                    behind(b, i, first)

            forward(0, True)
            with pe.Fori(1, B) as b:
                forward(b, False)
            for i in range(4):
                behind(B, i, False)
            column_dft(B - 1, 1, 1)

            pe.wait_ge(sums_ready, 1)
            nc.tensor.matmul(ps[0][:, 0:16 * B], table("ones"), sumsq[:, :], start=True, stop=True)
            nc.tensor.matmul(ps[1][:, 0:C * B], table("dc", 0, 64),
                             X[0:64].rearrange("k b (c m) -> k b c m", m=M)[:, :, :, 0],
                             start=True, stop=True).then_inc(sums_done, 1)

            pe.wait_ge(xc_scaled, 1)
            pe.wait_ge(spec_in, 16 * 32)
            for e in range(16):
                wait(pe, o_copied, e - 1)
                for kx in range(16):
                    for q in range(4):
                        rows = slice(32 * q, 32 * q + 32)
                        at = BANK * e + C * kx
                        last = nc.tensor.matmul(ps[4 * (e % 2) + q][32 * q:32 * q + 16, C * kx:C * (kx + 1)],
                                                XC[rows, :, 16 * e + kx], spec[rows, at:at + C],
                                                start=True, stop=True)
                last.then_inc(mix_done, 1)

            idft_h = table("idft_h")
            n = 0
            for i in range(4):
                pe.wait_ge(lv_signed, i + 1)
                for half in range(2):
                    for d in range(C):
                        wait(pe, v_copied_dve if n % 2 else v_copied_act, n // 2 - 1)
                        nc.tensor.matmul(ps[n % 4][:, 0:VH], LV[i % 2][:, :, d],
                                         idft_h[:, VH * half:VH * (half + 1)],
                                         start=True, stop=True).then_inc(v_done, 1)
                        n += 1

            pe.wait_ge(sums_ready, 2)
            nc.tensor.matmul(ps[4][:, 0:C * B], table("cross", 0, 64), R1[0:64, :], start=True, stop=False)
            nc.tensor.matmul(ps[4][:, 0:C * B], table("power", 0, 64), R2[0:64, :], start=False, stop=False)
            nc.tensor.matmul(ps[4][:, 0:C * B], table("power0", 0, 64), R3[0:64, :], start=False, stop=True)
            nc.tensor.matmul(ps[5][:, 0:C * B], table("dc", 0, 64),
                             O[0:64, :, 0:C], start=True, stop=True).then_inc(sums_done, 1)

            def column_idft(n, c, slot, q, g):
                if q == 0 and g == 0:
                    pe.wait_ge(v_low, c + 1)
                wait(pe, x1_done, 2 * (n - 1) + g + 1)
                for part in range(2):
                    last = nc.tensor.matmul(ps[g][:, :], W_parts[part][:, P * q:P * (q + 1)],
                                            V_parts[slot % 2][:, BANK * g:BANK * (g + 1)],
                                            start=(part == 0), stop=(part == 1))
                last.then_inc(y_done, 1)

            def transpose_x1(n, slot, q, k):
                wait(pe, gx_done, 2 * (n - 1) + k + 1)
                for h in range(CH):
                    last = nc.tensor.transpose(ps[2 + k][:, P * h:P * (h + 1)], x1[slot][:, 2 * q + k, h, :], ident)
                last.then_inc(t_done, 1)

            def convolve(t, g):
                pe.wait_ge(u_done, 2 * t + g + 1)
                wait(pe, r_done, 2 * (t - 1) + g + 1)
                bank = ps[4 + g]
                for m, shift in ((0, 0), (2, 1), (1, 1), (3, 2)):
                    half = m // 2
                    last = nc.tensor.matmul(bank[64 * half:64 * half + 64, :], conv[:, m, :],
                                            u[g][:, :, shift:shift + P], start=(m % 2 == 0) if half == 0 else (m == 2),
                                            stop=(m % 2 == 1))
                last.then_inc(conv_done, 1)

            def transpose_r(t, t_slot, g):
                pe.wait_ge(r_done, 2 * t + g + 1)
                wait(pe, out_done, 2 * (t - 1) + g + 1)
                for b in range(BG):
                    last = nc.tensor.transpose(ps[6 + g][:, P * b:P * (b + 1)],
                                               r[g][t_slot % 2][:, P * b:P * (b + 1)], ident)
                last.then_inc(rt_done, 1)

            def prep_t(n, s):
                slot, q = s // 4, s % 4
                if q == 0:
                    pe.wait_ge(x1_done, 2 * n + 8)
                for k in range(2):
                    transpose_x1(n, slot % 4, q, k)

            pe.wait_ge(w_low, 1)
            for n in range(9):
                for g in range(G):
                    column_idft(n, n // 4, n // 4, n % 4, g)
            for n in range(5):
                prep_t(n, n)

            def steps(it):
                known = isinstance(it, int)
                for s in range(STEPS):
                    t = STEPS * it + s
                    slot, q = (s + 9) // 4, (s + 9) % 4
                    for g in range(G):
                        convolve(t, g)
                        if g == 1:
                            transpose_r(t, s, 0)
                        elif not (known and t == 0):
                            transpose_r(t - 1, s - 1, 1)
                        if not (known and t + 9 >= H):
                            column_idft(t + 9, 4 * it + slot, slot, q, g)
                    if not (known and t + 5 >= H):
                        prep_t(t + 5, s + 5)

            pe.wait_ge(conv_in, 16 * 20)
            steps(0)
            with pe.Fori(1, H // STEPS - 1) as it:
                steps(it)
            steps(H // STEPS - 1)
            transpose_r(H - 1, STEPS - 1, 1)

        @block.scalar
        def _(act):
            act.wait_ge(tables_in, 16)
            nc.scalar.activation(W_parts[0][:, :], table("idft_w"), ACT.Copy).then_inc(w_high, 1)

            def squares(b):
                for i in range(TILES):
                    act.wait_ge(tile_in[i % 2], XT_USE * (TILES // 2 * b + i // 2 + 1))
                    flat = tile[i % 2].rearrange("p hh (w c) -> p (hh w) c", c=C)
                    for g in range(SQ_ACT):
                        at = (b * TILES + i) * 16 + g
                        if g == 1:
                            wait(act, squared, 2 * (b * TILES + i))
                        else:
                            wait(act, sq_act, (SQ_ACT - 1) * (b * TILES + i) + max(g - 1, 0))
                        ins = nc.scalar.activation(squares_act[g % 2], flat[:, :, 2 * g:2 * g + 2], ACT.Square,
                                                   accum_out=sq[:, bass.ds(at, 1)])
                        if g < SQ_ACT - 1:
                            ins.then_inc(sq_act, 1)
                        else:
                            ins.then_inc(squared, 2)

            squares(0)
            with act.Fori(1, B) as b:
                squares(b)

            act.wait_ge(var_ready, 1)
            nc.scalar.activation(small[:, 3, :], small[:, 2, :], ACT.Sqrt).then_inc(root_done, 1)

            def evac(s, e):
                act.wait_ge(mix_done, e + s + 1)
                for q in range(4):
                    dst = O_part[32 * q:32 * q + 16, bass.ds(BANK * (e + s), BANK)]
                    last = nc.scalar.activation(dst, ps[4 * s + q][32 * q:32 * q + 16, :], ACT.Copy)
                last.then_inc(o_copied, 1)

            with act.Fori(0, 8) as it:
                for s in range(2):
                    evac(s, 2 * it)

            for n in range(8):
                if n >= 2:
                    act.wait_ge(v_stored[n % 2], 32 * (n // 2))
                for d in range(0, C, 2):
                    act.wait_ge(v_done, C * n + d + 1)
                    nc.scalar.activation(VS[n % 2][:, :, d], ps[d % 4][:, 0:VH], ACT.Copy).then_inc(v_copied_act, 1)

            act.wait_ge(var_ready, 2)
            nc.scalar.activation(small[:, 9, :], small[:, 8, :], ACT.Sqrt).then_inc(root_done, 1)

            def relu(t, t_slot, g):
                if isinstance(t, int) and t == H - 1:
                    act.wait_ge(conv_done, 2 * t + g + 1)
                else:
                    act.wait_ge(u_done, 2 * t + g + 3)
                wait(act, rt_done, 2 * (t - 2) + g + 1)
                nc.scalar.activation(r[g][t_slot % 2], ps[4 + g][:, :], ACT.Relu, bias=bias[:, 0:1]).then_inc(r_done, 1)

            def normalise(n, s):
                slot, q = s // 4, s % 4
                if q == 0:
                    wait(act, u_done, 2 * n - 8)
                for k in range(2):
                    b = 2 * q + k
                    act.wait_ge(t_done, 2 * n + k + 1)
                    nc.scalar.activation(gx[slot % 2][:, b], ps[2 + k][:, :].rearrange("p (h j) -> p h j", h=CH),
                                         ACT.Identity, scale=small[:, 11, b:b + 1],
                                         bias=small[:, 13, b:b + 1]).then_inc(gx_done, 1)

            def spectra_high(c, slot):
                wait(act, y_done, 8 * c - 8)
                act.wait_ge(vc_in[slot % 2], 32 * (slot // 2 + 1) + 16 * (c - slot))
                nc.scalar.activation(V_parts[slot % 2][:, :], Vc[slot % 2][:, :], ACT.Copy).then_inc(v_high, 1)

            act.wait_ge(norm1_ready, 1)
            act.wait_ge(bias_in, 64)
            for c in range(4):
                spectra_high(c, c)
            for n in range(5):
                normalise(n, n)

            def steps(it):
                known = isinstance(it, int)
                for s in range(STEPS):
                    t = STEPS * it + s
                    relu(t, s, 0)
                    relu(t, s, 1)
                    if not (known and t + 5 >= H):
                        normalise(t + 5, s + 5)
                    if (s + 9) % 4 == 0 and not (known and t + 13 >= H):
                        slot = (s + 13) // 4
                        spectra_high(4 * it + slot, slot)

            steps(0)
            with act.Fori(1, H // STEPS - 1) as it:
                steps(it)
            steps(H // STEPS - 1)

        @block.vector
        def _(dve):
            chain = [0]

            def link(ins):
                chain[0] += 1
                ins.then_inc(dve_step, 1)
                dve.wait_ge(dve_step, chain[0])

            dve.wait_ge(tables_in, 16)
            dve.wait_ge(w_high, 1)
            nc.vector.tensor_tensor(W_parts[1][:, :], table("idft_w"), W_parts[0][:, :].bitcast(F32),
                                    ALU.subtract).then_inc(w_low, 1)

            def copy_zt(b, sub, m):
                dve.wait_ge(zt_done, 16 * b + 8 * sub + m + 1)
                wait(dve, coldft_done, 4 * b + 2 * sub + m // 4 - 1)
                nc.vector.tensor_copy(ZT[:, 4 * m:4 * m + 4, :],
                                      ps[4 + m % 2][:, :].rearrange("p (c k) -> p c k", c=4)).then_inc(zt_copied, 1)

            def copy_modes(b, e):
                dve.wait_ge(coldft_done, 4 * b + e + 3)
                dst = X[0:64, bass.ds(b, 1), BANK * e:BANK * (e + 1)].rearrange("p b n -> p (b n)")
                nc.vector.tensor_copy(dst, ps[6 + e][0:64, :]).then_inc(x_copied, 1)

            def behind(b, i, first):
                if first and i < 4:
                    return
                prev, sub = (b - 1, 1) if i < 4 else (b, 0)
                for m in (2 * (i % 4), 2 * (i % 4) + 1):
                    copy_zt(prev, sub, m)
                if not first and i in (3, 5):
                    copy_modes(b - 1, (i - 3) // 2)

            def forward(b, first):
                for i in range(TILES):
                    dve.wait_ge(tile_in[i % 2], XT_USE * (TILES // 2 * b + i // 2 + 1))
                    flat = tile[i % 2].rearrange("p hh (w c) -> p (hh w) c", c=C)
                    for g in range(SQ_ACT, 16):
                        at = (b * TILES + i) * 16 + g
                        v = flat[:, :, 2 * g:2 * g + 2]
                        n = (b * TILES + i) * SQ_DVE + g - SQ_ACT
                        wait(dve, sq_dve, n - 1)
                        nc.vector.scalar_tensor_tensor(squares_dve[g % 2], v, 1.0, v, ALU.mult, ALU.mult,
                                                       accum_out=sq[:, bass.ds(at, 1)]).then_inc(sq_dve, 1)
                    for blk in range(2):
                        dve.wait_ge(rowdft_done, 2 * TILES * b + 2 * i + blk + 1)
                        at = i * TW + 16 * blk
                        nc.vector.tensor_copy(Z[:, :, at:at + 16],
                                              ps[(2 * i + blk) % 4][:, :].rearrange("p (w c) -> p c w", c=C)
                                              ).then_inc(z_copied, 1)
                    behind(b, i, first)

            forward(0, True)
            with dve.Fori(1, B) as b:
                forward(b, False)
            for i in range(4):
                behind(B, i, False)
            copy_modes(B - 1, 1)

            dve.wait_ge(bias_in, 64)
            link(nc.vector.tensor_scalar(neg_bias[:, :], bias[:, :], -1.0, None, ALU.mult))
            dve.wait_ge(squared, 2 * B * TILES)
            dve.wait_ge(sq_act, (SQ_ACT - 1) * B * TILES)
            dve.wait_ge(sq_dve, SQ_DVE * B * TILES)
            nc.vector.tensor_reduce(sumsq[:, :].rearrange("p (b g) -> p b g", b=B),
                                    sq[:, :].rearrange("p (b t g) -> p b g t", b=B, g=16),
                                    AX.X, ALU.add).then_inc(sums_ready, 1)
            dve.wait_ge(sums_done, 1)

            def group_sum(dst, bank, n, mask):
                v = masked[:, 0:B * n].rearrange("p (b g) -> p b g", b=B)
                m = table(mask).rearrange("p (b g) -> p b g", b=1).broadcast_to([P, B, n])
                link(nc.vector.tensor_tensor(v, bank[:, 0:B * n].rearrange("p (b g) -> p b g", b=B), m, ALU.mult))
                link(nc.vector.tensor_reduce(dst, v, AX.X, ALU.add))

            def variance(total, total_sq, mean, var, tmp):
                link(nc.vector.tensor_scalar(mean, total, 1.0 / N2, None, ALU.mult))
                link(nc.vector.tensor_tensor(tmp, mean, mean, ALU.mult))
                link(nc.vector.scalar_tensor_tensor(var, total_sq, 1.0 / N2, tmp, ALU.mult, ALU.subtract))
                nc.vector.tensor_scalar(var, var, 0.0, GN_EPS, ALU.max, ALU.add).then_inc(var_ready, 1)

            def reciprocal_root(var, root, tmp, dst):
                link(nc.vector.reciprocal(tmp, root))
                link(nc.vector.tensor_tensor(tmp, tmp, var, ALU.mult))
                link(nc.vector.tensor_tensor(tmp, tmp, root, ALU.add))
                link(nc.vector.tensor_scalar(tmp, tmp, 0.5, None, ALU.mult))
                link(nc.vector.reciprocal(dst, tmp))

            group_sum(small[:, 0, :], ps[0], 16, "same_group16")
            group_sum(small[:, 1, :], ps[1], 32, "same_group32")
            variance(small[:, 1, :], small[:, 0, :], small[:, 5, :], small[:, 2, :], small[:, 4, :])
            dve.wait_ge(root_done, 1)
            reciprocal_root(small[:, 2, :], small[:, 3, :], small[:, 4, :], small[:, 6, :])
            dve.wait_ge(xc_in, 16 * 32)
            zero_mode = XC[0:32, :, 0].rearrange("p (b ri) -> p b ri", ri=2)[:, :, 0]
            link(nc.vector.scalar_tensor_tensor(zero_mode, small[0:32, 1, :], -0.5, zero_mode, ALU.mult, ALU.add))
            for b in range(B):
                ins = nc.vector.tensor_scalar(XC[:, 2 * b:2 * b + 2, :], XC[:, 2 * b:2 * b + 2, :],
                                              small[:, 6, b:b + 1], None, ALU.mult)
            ins.then_inc(xc_scaled, 1)

            for i in range(4):
                dve.wait_ge(lv_in[i % 2], 128 * (i // 2 + 1))
                for s in range(2):
                    v = LV[i % 2][64 * s + 32:64 * s + 64, 64 * s:64 * s + 32, :]
                    ins = nc.vector.tensor_scalar(v, v, -1.0, None, ALU.mult)
                ins.then_inc(lv_signed, 1)
                if i == 0:
                    dve.wait_ge(o_in, 32)
                for half in range(2):
                    m = 2 * i + half
                    if m >= 2:
                        dve.wait_ge(v_stored[m % 2], 32 * (m // 2))
                    for d in range(1, C, 2):
                        dve.wait_ge(v_done, C * m + d + 1)
                        nc.vector.tensor_copy(VS[m % 2][:, :, d], ps[d % 4][:, 0:VH]).then_inc(v_copied_dve, 1)
                    b = m
                    pr = prod[0:64, 0:C * M].rearrange("p (c m) -> p c m", m=M)
                    o_t = O[0:64, b].rearrange("p (m c) -> p c m", c=C)
                    link(nc.vector.tensor_tensor(pr, X[0:64, b].rearrange("p (c m) -> p c m", m=M), o_t, ALU.mult))
                    link(nc.vector.tensor_reduce(R1[0:64, C * b:C * (b + 1)], pr, AX.X, ALU.add))
                    link(nc.vector.tensor_tensor(pr, o_t, o_t, ALU.mult))
                    nc.vector.tensor_copy(R3[0:64, C * b:C * (b + 1)], pr[:, :, 0])
                    ins = nc.vector.tensor_reduce(R2[0:64, C * b:C * (b + 1)], pr, AX.X, ALU.add)
                    if b < B - 1:
                        link(ins)
            ins.then_inc(sums_ready, 1)
            dve.wait_ge(sums_done, 2)
            group_sum(small[:, 7, :], ps[4], 32, "same_group32")
            link(nc.vector.tensor_tensor(small[:, 7, :], small[:, 7, :], small[:, 0, :], ALU.add))
            group_sum(small[:, 10, :], ps[5], 32, "same_group32")
            link(nc.vector.tensor_tensor(small[:, 10, :], small[:, 10, :], small[:, 1, :], ALU.add))
            variance(small[:, 10, :], small[:, 7, :], small[:, 12, :], small[:, 8, :], small[:, 4, :])
            dve.wait_ge(root_done, 2)
            reciprocal_root(small[:, 8, :], small[:, 9, :], small[:, 4, :], small[:, 11, :])
            link(nc.vector.tensor_tensor(small[:, 13, :], small[:, 12, :], small[:, 11, :], ALU.mult))
            link(nc.vector.tensor_scalar(small[:, 13, :], small[:, 13, :], -1.0, bias[:, 0:1], ALU.mult, ALU.add))
            for g in range(G):
                nc.vector.memset(u[g][:, :, 0:1], 0.0)
                ins = nc.vector.memset(u[g][:, :, 129:130], 0.0)
            ins.then_inc(norm1_ready, 1)

            def spectra_low(c, slot):
                dve.wait_ge(v_high, c + 1)
                low = V_parts[slot % 2][64:128, :]
                nc.vector.tensor_tensor(low, Vc[slot % 2][64:128, :], low.bitcast(F32), ALU.subtract).then_inc(v_low, 1)

            def add_y(n, s, it, g):
                slot, q = s // 4, s % 4
                if q == 0 and g == 0:
                    dve.wait_ge(xin_in[slot % 2], 128 * (slot // 2 + 1) + 256 * it)
                    wait(dve, stored[slot % 4], 128 * (slot // 4) + 128 * it)
                dve.wait_ge(y_done, 2 * n + g + 1)
                src = x_in[slot % 2][:, BG * g:BG * (g + 1), :, C * q:C * (q + 1)]
                dst = x1[slot % 4][:, BG * g:BG * (g + 1), :, C * q:C * (q + 1)]
                y = ps[g][:, :].rearrange("p (b h c) -> p b h c", b=BG, h=CH)
                nc.vector.tensor_tensor(dst, y, src, ALU.add).then_inc(x1_done, 1)

            def next_u(t, s, g):
                slot, row = (s + 1) // 4, (s + 1) % 4
                dve.wait_ge(conv_done, 2 * t + g + 1)
                if row == 0:
                    dve.wait_ge(gx_done, 2 * (t + 1) + 4 * g + 4)
                nc.vector.scalar_tensor_tensor(
                    u[g][:, :, 1:129], ps[4 + g][:, :].rearrange("p (b j) -> p b j", b=BG), neg_bias[:, 0:1],
                    gx[slot % 2][:, BG * g:BG * (g + 1), row, :], ALU.max, ALU.add).then_inc(u_done, 1)

            def add_r(t, s, g):
                dve.wait_ge(rt_done, 2 * t + g + 1)
                v = x1[s // 4 % 4][:, BG * g:BG * (g + 1), s % 4, :]
                nc.vector.tensor_tensor(v, ps[6 + g][:, :].rearrange("p (b n) -> p b n", b=BG), v,
                                        ALU.add).then_inc(out_done, 1)

            for n in range(9):
                if n % 4 == 0:
                    spectra_low(n // 4, n // 4)
                for g in range(G):
                    add_y(n, n, 0, g)
            spectra_low(3, 3)
            for g in range(G):
                dve.wait_ge(gx_done, 4 * g + 4)
                nc.vector.tensor_scalar(u[g][:, :, 1:129], gx[0][:, BG * g:BG * (g + 1), 0, :],
                                        bias[:, 0:1], None, ALU.subtract).then_inc(u_done, 1)

            def steps(it):
                known = isinstance(it, int)
                for s in range(STEPS):
                    t = STEPS * it + s
                    for g in range(G):
                        if not (known and t + 1 >= H):
                            next_u(t, s, g)
                        if g == 1:
                            add_r(t, s, 0)
                        elif not (known and t == 0):
                            add_r(t - 1, s + STEPS - 1, 1)
                        if not (known and t + 9 >= H):
                            add_y(t + 9, s + 9, it, g)
                    if (s + 9) % 4 == 0 and not (known and t + 13 >= H):
                        slot = (s + 13) // 4
                        spectra_low(4 * it + slot, slot)

            steps(0)
            with dve.Fori(1, H // STEPS - 1) as it:
                steps(it)
            steps(H // STEPS - 1)
            add_r(H - 1, STEPS - 1, 1)


_INS = ["x", "L0_conv_W", "L1_conv_w", "L1_conv_b"]


def kernel(**inputs):
    import numpy as _np
    import concourse.bacc as _bacc
    from concourse import mybir as _mybir
    from concourse.bass_utils import run_bass_kernel_spmd as _run

    nc = _bacc.Bacc("TRN2", target_bir_lowering=False, num_devices=1)
    shape = inputs["x"].shape
    arrays, args = {}, []
    named = [(name, _np.ascontiguousarray(inputs[name])) for name in _INS]
    for name, a in named + [("tables", tables(shape[1], shape[2]))]:
        arrays[f"in_{name}_dram"] = a
        args.append(nc.dram_tensor(f"in_{name}_dram", a.shape, _mybir.dt.from_np(a.dtype), kind="ExternalInput").ap())
    args.append(nc.dram_tensor("out_0_dram", shape, _mybir.dt.float32, kind="ExternalOutput").ap())
    conv_preact_pair(nc, *args)
    r = _run(nc, [arrays], core_ids=[0])
    return r.results[0]["out_0_dram"]
```

```python
from contextlib import ExitStack

import concourse.bass as bass
import numpy as np
from concourse import mybir

F32 = mybir.dt.float32
F32R = mybir.dt.float32r
ALU = mybir.AluOpType
ACT = mybir.ActivationFunctionType
AX = mybir.AxisListType

P = 128
BANK = 512
M = 32
GN_EPS = 1e-5


def table_layout(H):
    sizes = [("dft_h", H // P * 64), ("dft_w", 2 * 4 * 64), ("idft_h", H), ("idft_w", 4 * P),
             ("ident", P), ("ones", P), ("dc", P), ("cross", P), ("power", P), ("power0", P),
             ("same_group16", 16), ("same_group32", 32)]
    at, cols = 0, {}
    for name, n in sizes:
        cols[name] = (at, n)
        at += n
    return cols, at


def tables(H, W):
    cols, total = table_layout(H)
    out = np.zeros((P, total))

    def put(name, rows, values):
        at, n = cols[name]
        out[rows, at:at + n] = values.reshape(values.shape[0], n)

    every = slice(0, P)
    p, k = np.arange(P), np.arange(M)
    h = (np.arange(H // P)[None, :] * P + p[:, None])[:, :, None] * k * (2 * np.pi / H)
    put("dft_h", every, np.concatenate([np.cos(h), np.sin(h)], -1))
    w = (np.arange(4)[None, :] * P + p[:, None])[:, :, None] * k * (2 * np.pi / W)
    put("dft_w", every, np.stack([np.concatenate([np.cos(w), -np.sin(w)], -1),
                                  np.concatenate([-np.sin(w), -np.cos(w)], -1)], 1))
    a = k[:, None] * np.arange(H) * (2 * np.pi / H)
    put("idft_h", every, np.concatenate([np.cos(a), np.sin(a)] * 2, 0))
    N = H * W
    twice = np.where(k == 0, 1.0, 2.0)
    pos = 4 * np.arange(P)[None, :] + np.arange(4)[:, None]
    a = k[:, None, None] * pos * (2 * np.pi / W)
    t = twice[:, None, None] / N * np.stack([np.cos(a), -np.sin(a)])
    t = t.reshape(64, 4 * P)
    put("idft_w", every, np.concatenate([t, t], 0))
    put("ident", every, np.eye(P))
    put("ones", every, np.ones((P, P)))
    rows = slice(0, 64)
    wide = np.ones((1, P))
    dc = np.zeros((64, 1))
    dc[0] = 1
    put("dc", rows, dc * wide)
    put("cross", rows, np.tile(2 * twice / N, 2)[:, None] * wide)
    put("power", rows, np.tile(np.where(k == 0, 0.5, 2.0) / N, 2)[:, None] * wide)
    p0 = np.zeros((64, 1))
    p0[0], p0[M] = 0.5 / N, -0.5 / N
    put("power0", rows, p0 * wide)
    group = (p % 32) // 2
    put("same_group16", every, (group[:, None] == np.arange(16)).astype(float))
    put("same_group32", every, (group[:, None] == np.arange(32) // 2).astype(float))
    return out.astype(np.float32)


def conv_preact_pair(nc, x, spec_w, conv_w, conv_b, tab, out):
    B, H, W, C = x.shape
    assert (B, W, C) == (8, 512, 32) and H % P == 0
    HH = H // P
    G = 2
    BG = B // G
    ROW = W * C
    TW = 32
    TILES = W // 2 // TW
    TILE = 2 * TW * C
    SQ_ACT = 10
    SQ_DVE = 16 - SQ_ACT
    CH = 4
    CHUNKS = H // CH
    V_DVE = C // 4
    V_ACT = C - V_DVE
    V_PART = B * CH * C // 4
    STEPS = 16
    SPECTRA = [(0, 0), (0, 1), (1, 0), (1, 1), (2, 0), (3, 0), (2, 1), (3, 1)]
    N2 = float(2 * H * W)

    x_tiles = x.rearrange("b (hh p) (half i w) c -> b i hh p half (w c)", p=P, half=2, i=TILES)
    x_rows = x.rearrange("b h (j q) c -> b j h (q c)", q=4)
    out_rows = out.rearrange("b h (j q) c -> b j h (q c)", q=4)
    X_dram = nc.dram_tensor("modes_in", (B, 64, C, M), F32, kind="Internal").ap()
    O_dram = nc.dram_tensor("modes_out", (2 * B, M, M, C), F32, kind="Internal").ap()
    V_dram = nc.dram_tensor("row_spectra", (CHUNKS, 64, B, CH * C), F32, kind="Internal").ap()

    ctx = ExitStack()
    with ctx:
        def sb(name, cols):
            return ctx.enter_context(nc.sbuf_tensor(name, [P, cols], F32))

        def sem(name):
            return ctx.enter_context(nc.semaphore(name))

        cols, total = table_layout(H)
        T = sb("tables", total)

        def table(name, lo=0, hi=P):
            at, n = cols[name]
            return T[lo:hi, at:at + n]

        KB = 256
        arena = sb("arena", 164 * KB)

        def region(kb, size_kb):
            return arena[:, kb * KB:(kb + size_kb) * KB]

        tile = [region(32 * s, 8 * HH).rearrange("p (hh n) -> p hh n", hh=HH) for s in range(2)]
        Z = region(64, 32).rearrange("p (c w) -> p c w", c=C)
        ZT = region(96, 16).rearrange("p (c k) -> p c k", c=C)
        X = region(128, 32).rearrange("p (b n) -> p b n", b=B)
        sq = sb("sq", B * TILES * 16)
        SQ = TILE * HH // 16
        squares_act = [region(160 + 2 * s, 2)[:, 0:SQ].rearrange("p (w c) -> p w c", c=2) for s in range(2)]
        squares_dve = [sb(f"squares_dve{s}", SQ).rearrange("p (w c) -> p w c", c=2) for s in range(2)]
        spec = region(0, 32)
        O_part = region(32, 32)
        XC = region(112, 16).rearrange("p (r n) -> p r n", r=2 * B)
        O = region(96, 32).rearrange("p (b n) -> p b n", b=B)
        LV = [region(64 + 16 * s, 16).rearrange("p (m d) -> p m d", d=C) for s in range(2)]
        VH = H // 2
        VS = [region(32 * s, H // 16).rearrange("p (h d) -> p h d", d=C) for s in range(2)]
        prod = region(160, 4)
        x_in = [region(64 + 16 * s, 16).rearrange("p (b h n) -> p b h n", b=B, h=CH) for s in range(2)]
        x1 = [region(16 * s, 16).rearrange("p (b h n) -> p b h n", b=B, h=CH) for s in range(4)]
        gx = [region(96 + 16 * s, 16).rearrange("p (b h n) -> p b h n", b=B, h=CH) for s in range(2)]
        Vc = [region(128 + 4 * s, 4) for s in range(2)]
        r = [[region(136 + 4 * g + 2 * s, 2) for s in range(2)] for g in range(G)]
        u = [arena[:, 144 * KB + g * BG * 130:144 * KB + (g + 1) * BG * 130]
             .rearrange("p (b j) -> p b j", b=BG) for g in range(G)]
        V_parts = [ctx.enter_context(nc.sbuf_tensor(f"V_parts{s}", [P, G * BANK], F32R)) for s in range(2)]
        W_parts = [ctx.enter_context(nc.sbuf_tensor(f"W_parts{s}", [P, 4 * P], F32R)) for s in range(2)]
        conv = sb("conv_w", 4 * 64).rearrange("p (m n) -> p m n", m=4)
        bias, neg_bias = sb("bias", 1), sb("neg_bias", 1)
        small = sb("small", 16 * B).rearrange("p (n b) -> p n b", b=B)
        sumsq = sb("sumsq", 16 * B)
        masked = sb("masked", C * B)
        R1, R2, R3 = sb("R1", C * B), sb("R2", C * B), sb("R3", C * B)
        ps = [ctx.enter_context(nc.psum_tensor(f"ps{i}", [P, BANK], F32)) for i in range(8)]

        tables_in, bias_in, conv_in = sem("tables_in"), sem("bias_in"), sem("conv_in")
        conv_zero = sem("conv_zero")
        spec_in = [sem(f"spec_in{k}") for k in range(8)]
        tile_in = [sem(f"tile_in{s}") for s in range(2)]
        sq_act, sq_dve, squared = sem("sq_act"), sem("sq_dve"), sem("squared")
        rowdft_done, z_copied = sem("rowdft_done"), sem("z_copied")
        zt_done, zt_copied = sem("zt_done"), sem("zt_copied")
        coldft_done, x_copied, x_stored = sem("coldft_done"), sem("x_copied"), sem("x_stored")
        last_x_stored, last_xc_in = sem("last_x_stored"), sem("last_xc_in")
        xc_in, xc_scaled = sem("xc_in"), sem("xc_scaled")
        dve_step, sums_ready, sums_done = sem("dve_step"), sem("sums_ready"), sem("sums_done")
        var_ready, root_done = sem("var_ready"), sem("root_done")
        mix_done, o_copied, o_stored = sem("mix_done"), sem("o_copied"), sem("o_stored")
        o_in, lv_zero, lv_signed = sem("o_in"), sem("lv_zero"), sem("lv_signed")
        lv_in = [sem(f"lv_in{s}") for s in range(2)]
        v_done, v_copied_act, v_copied_dve = sem("v_done"), sem("v_copied_act"), sem("v_copied_dve")
        v_stored = [sem(f"v_stored{s}") for s in range(2)]
        norm1_ready = sem("norm1_ready")
        xin_in = [sem(f"xin_in{s}") for s in range(2)]
        vc_in = [sem(f"vc_in{s}") for s in range(2)]
        w_high, w_low, v_high, v_low = sem("w_high"), sem("w_low"), sem("v_high"), sem("v_low")
        y_done, x1_done, t_done, gx_done = sem("y_done"), sem("x1_done"), sem("t_done"), sem("gx_done")
        u_done, conv_done, r_done, rt_done = sem("u_done"), sem("conv_done"), sem("r_done"), sem("rt_done")
        out_done = sem("out_done")
        stored = [sem(f"stored{s}") for s in range(4)]

        def wait(eng, s, value):
            if not isinstance(value, int) or value > 0:
                eng.wait_ge(s, value)

        XT_USE = 16 * HH

        def turn_modes(eng, b, written, count, read):
            eng.wait_ge(x_copied, 2 * b + 2)
            eng.dma_start(X_dram[bass.ds(b, 1)].rearrange("b k c m -> k b (c m)"),
                          X[0:64, bass.ds(b, 1), :]).then_inc(written, 16)
            eng.wait_ge(written, 16 * count)
            for q in range(4):
                for ri in range(2):
                    src = X_dram[bass.ds(b, 1), 32 * ri + 8 * q:32 * ri + 8 * q + 8][0]
                    dst = XC[32 * q:32 * q + 32, bass.ds(2 * b + ri, 1), :].rearrange("c r (k m) -> c (r k) m", k=8)
                    eng.dma_start(dst, src.rearrange("k c m -> c k m")).then_inc(read, 16)

        block = ctx.enter_context(nc.Block())

        @block.sync
        def _(sp):
            sp.dma_start(T[:, :], tab).then_inc(tables_in, 16)

            def load_tiles(b, first):
                for i in range(TILES):
                    if not (first and i < 2):
                        sp.wait_ge(squared, 2 * TILES * b + 2 * (i - 1))
                        sp.wait_ge(z_copied, 2 * TILES * b + 2 * (i - 1))
                    for hh in range(HH):
                        dst = tile[i % 2][:, hh, :].rearrange("p (half n) -> p half n", half=2)
                        src = x_tiles[b, i, hh] if first else x_tiles[bass.ds(b, 1), i, hh, :, :, :][0]
                        sp.dma_start(dst, src).then_inc(tile_in[i % 2], 16)

            load_tiles(0, True)
            with sp.Fori(1, B) as b:
                load_tiles(b, False)

            sp.wait_ge(squared, 2 * (B * TILES - 1))
            sp.wait_ge(z_copied, 2 * (B * TILES - 1))
            for k in range(8):
                for q in range(4):
                    src = spec_w[:, 8 * q + k].rearrange("kx c d -> c kx d")
                    sp.dma_start(spec[32 * q:32 * q + 32, k * 1024:(k + 1) * 1024]
                                 .rearrange("c (kx d) -> c kx d", d=C), src).then_inc(spec_in[k], 16)
            turn_modes(sp, B - 1, last_x_stored, 1, last_xc_in)
            for part in range(2):
                sp.wait_ge(o_copied, 8 * (part + 1))
                for q in range(4):
                    at = 8 * q + 4 * part
                    sp.dma_start(O_dram[:, at:at + 4].rearrange("r k m d -> r (k m d)"),
                                 O_part[32 * q:32 * q + 16, 4096 * part:4096 * (part + 1)]).then_inc(o_stored, 16)
            sp.wait_ge(o_stored, 128)
            sp.wait_ge(lv_zero, 1)

            def load_pair(i):
                for s in range(2):
                    b = 2 * i + s
                    src = O_dram[2 * b:2 * b + 2].rearrange("ri ky kx d -> ri kx ky d")
                    for part in range(2):
                        for ri in range(2):
                            rows = 64 * s + 32 * part
                            m = 64 * s + 32 * (ri ^ part)
                            sp.dma_start(LV[i % 2][rows:rows + 32, m:m + 32, :], src[ri]).then_inc(lv_in[i % 2], 16)

            load_pair(0)
            for ri in range(2):
                sp.dma_start(O[32 * ri:32 * ri + 32],
                             O_dram.rearrange("(b ri) ky kx d -> ri ky b (kx d)", ri=2)[ri]).then_inc(o_in, 16)
            load_pair(1)

            def store_row_spectra(n):
                i, half = SPECTRA[n]
                sp.wait_ge(v_copied_act, V_ACT * (n + 1))
                sp.wait_ge(v_copied_dve, V_DVE * (n + 1))
                for s in range(2):
                    dst = V_dram[VH // CH * half:VH // CH * (half + 1), :, 2 * i + s].rearrange("n k m -> k n m")
                    sp.dma_start(dst, VS[n % 2][64 * s:64 * s + 64].rearrange("k (n h) d -> k n (h d)", h=CH)
                                 ).then_inc(v_stored[n % 2], 16)

            for n in range(6):
                store_row_spectra(n)
                if n in (1, 3):
                    load_pair(n // 2 + 2)

            def load_spectra(c, slot):
                wait(sp, v_low, 4 * (c - 1))
                sp.wait_ge(sums_ready, 2)
                for part in range(2):
                    src = V_dram[bass.ds(c, 1)][0].rearrange("k b m -> k (b m)")
                    sp.dma_start(Vc[slot % 2][64 * part:64 * part + 64, :], src).then_inc(vc_in[slot % 2], 16)

            def load_rows(c, slot):
                wait(sp, x1_done, 8 * c - 8)
                for b in range(B):
                    sp.dma_start(x_in[slot % 2][:, b], x_rows[b, :, bass.ds(CH * c, CH), :]
                                 ).then_inc(xin_in[slot % 2], 16)

            def store_chunk(c, c_slot):
                sp.wait_ge(out_done, 8 * c + 8)
                sp.wait_ge(norm1_ready, 1)
                for b in range(B):
                    sp.dma_start(out_rows[b, :, bass.ds(CH * c, CH), :], x1[c_slot][:, b]
                                 ).then_inc(stored[c_slot], 16)

            for s in range(2):
                sp.wait_ge(v_stored[s], 3 * 32)
            load_spectra(0, 0)
            load_spectra(1, 1)
            store_row_spectra(6)
            load_rows(0, 0)
            store_row_spectra(7)
            load_rows(1, 1)
            for s in range(2):
                sp.wait_ge(v_stored[s], 4 * 32)
            for c in range(2, 4):
                load_spectra(c, c)
                load_rows(c, c)
            load_spectra(4, 4)
            with sp.Fori(0, CHUNKS // 4 - 2) as it:
                for s in range(4):
                    load_spectra(4 * it + (s + 5), s + 1)
                    load_rows(4 * it + (s + 4), s)
                    store_chunk(4 * it + s, s)
            for c in range(CHUNKS - 8, CHUNKS - 4):
                if c + 5 < CHUNKS:
                    load_spectra(c + 5, c + 5)
                load_rows(c + 4, c)
                store_chunk(c, c % 4)
            for s in range(4):
                store_chunk(CHUNKS - 4 + s, s)
            for s in range(4):
                sp.wait_ge(stored[s], 128 * (CHUNKS // 4))

        @block.gpsimd
        def _(pool):
            nc.gpsimd.memset(conv[:, :, :], 0.0).then_inc(conv_zero, 1)
            pool.wait_ge(conv_zero, 1)
            n = 0
            for m, (shift, first) in enumerate(((-4, 0), (0, 0), (0, 2), (4, 2))):
                for i in range(4):
                    for o in range(first, first + 2):
                        tap = i + shift - o + 2
                        if 0 <= tap < 5:
                            pool.dma_start(conv[32 * i:32 * i + 32, m, 32 * (o % 2):32 * (o % 2) + 32],
                                           conv_w[:, tap, 0, :]).then_inc(conv_in, 16)
                            n += 1
            assert n == 20
            for i in range(4):
                pool.dma_start(bias[32 * i:32 * i + 32, :], conv_b.rearrange("(c n) -> c n", n=1)).then_inc(bias_in, 16)
            with pool.Fori(0, B - 1) as b:
                turn_modes(pool, b, x_stored, b + 1, xc_in)
            pool.wait_ge(coldft_done, 4 * B)
            for s in range(2):
                nc.gpsimd.memset(LV[s][0:64, 64:128, :], 0.0)
                last = nc.gpsimd.memset(LV[s][64:128, 0:64, :], 0.0)
            last.then_inc(lv_zero, 1)

        @block.tensor
        def _(pe):
            pe.wait_ge(tables_in, 16)
            dft_h = table("dft_h").rearrange("p (hh k) -> p hh k", hh=HH)
            dft_w = table("dft_w").rearrange("p (s w k) -> p s w k", s=2, w=4)
            ident = table("ident")

            def row_dft(b, i):
                pe.wait_ge(tile_in[i % 2], XT_USE * (TILES // 2 * b + i // 2 + 1))
                for blk in range(2):
                    n = 2 * TILES * b + 2 * i + blk
                    wait(pe, z_copied, n - 3)
                    for hh in range(HH):
                        for half in range(2):
                            at = half * TW * C + blk * BANK
                            last = nc.tensor.matmul(ps[(2 * i + blk) % 4][64 * half:64 * half + 64, :],
                                                    dft_h[:, hh, :], tile[i % 2][:, hh, at:at + BANK],
                                                    start=(hh == 0), stop=(hh == HH - 1))
                    last.then_inc(rowdft_done, 1)

            def transpose_z(b, sub, m):
                if m == 0:
                    pe.wait_ge(z_copied, 16 * b + 8 * sub + 8)
                wait(pe, zt_copied, 16 * b + 8 * sub + m - 1)
                for c in range(4):
                    last = nc.tensor.transpose(ps[4 + m % 2][:, P * c:P * (c + 1)],
                                               Z[:, 4 * m + c, P * sub:P * (sub + 1)], ident)
                last.then_inc(zt_done, 1)

            def column_dft(b, sub, e):
                pe.wait_ge(zt_copied, 16 * b + 8 * sub + 4 * e + 4)
                if sub == 0:
                    wait(pe, x_copied, 2 * b + e - 1)
                for k in range(4):
                    half, cs = k // 2, k % 2
                    at = 64 * half + 32 * cs
                    last = nc.tensor.matmul(ps[6 + e][0:64, :], dft_w[:, cs, 2 * half + sub, :],
                                            ZT[:, 16 * e:16 * e + 16, at:at + 32],
                                            start=(sub == 0 and k == 0), stop=(sub == 1 and k == 3))
                last.then_inc(coldft_done, 1)

            def behind(b, i, first):
                if first and i < 4:
                    return
                if i == 0:
                    column_dft(b - 1, 0, 1)
                if i == 4 and not first:
                    column_dft(b - 1, 1, 1)
                prev, sub = (b - 1, 1) if i < 4 else (b, 0)
                for m in (2 * (i % 4), 2 * (i % 4) + 1):
                    transpose_z(prev, sub, m)
                if i % 4 == 2:
                    column_dft(prev, sub, 0)

            def forward(b, first):
                for i in range(TILES):
                    row_dft(b, i)
                    behind(b, i, first)

            forward(0, True)
            with pe.Fori(1, B) as b:
                forward(b, False)
            for i in range(4):
                behind(B, i, False)
            column_dft(B - 1, 1, 1)

            pe.wait_ge(sums_ready, 1)
            nc.tensor.matmul(ps[0][:, 0:16 * B], table("ones"), sumsq[:, :], start=True, stop=True)
            nc.tensor.matmul(ps[1][:, 0:C * B], table("dc", 0, 64),
                             X[0:64].rearrange("k b (c m) -> k b c m", m=M)[:, :, :, 0],
                             start=True, stop=True).then_inc(sums_done, 1)

            pe.wait_ge(xc_scaled, 1)
            for e in range(16):
                if e % 2 == 0:
                    pe.wait_ge(spec_in[e // 2], 64)
                wait(pe, o_copied, e - 1)
                for kx in range(16):
                    for q in range(4):
                        rows = slice(32 * q, 32 * q + 32)
                        at = BANK * e + C * kx
                        last = nc.tensor.matmul(ps[4 * (e % 2) + q][32 * q:32 * q + 16, C * kx:C * (kx + 1)],
                                                XC[rows, :, 16 * e + kx], spec[rows, at:at + C],
                                                start=True, stop=True)
                last.then_inc(mix_done, 1)

            idft_h = table("idft_h")
            def row_idft(step):
                i, half = SPECTRA[step]
                pe.wait_ge(lv_signed, i + 1)
                for d in range(C):
                    n = C * step + d
                    if n % 4 == 3:
                        wait(pe, v_copied_dve, n // 4)
                    else:
                        wait(pe, v_copied_act, 3 * (n // 4 - 1) + n % 4 + 1)
                    nc.tensor.matmul(ps[n % 4][:, 0:VH], LV[i % 2][:, :, d],
                                     idft_h[:, VH * half:VH * (half + 1)],
                                     start=True, stop=True).then_inc(v_done, 1)

            for step in range(5):
                row_idft(step)
            pe.wait_ge(sums_ready, 2)
            nc.tensor.matmul(ps[4][:, 0:C * B], table("cross", 0, 64), R1[0:64, :], start=True, stop=False)
            nc.tensor.matmul(ps[4][:, 0:C * B], table("power", 0, 64), R2[0:64, :], start=False, stop=False)
            nc.tensor.matmul(ps[4][:, 0:C * B], table("power0", 0, 64), R3[0:64, :], start=False, stop=True)
            nc.tensor.matmul(ps[5][:, 0:C * B], table("dc", 0, 64),
                             O[0:64, :, 0:C], start=True, stop=True).then_inc(sums_done, 1)
            for step in range(5, 8):
                row_idft(step)

            def column_idft(n, c, slot, q, g):
                if q == 0 and g == 0:
                    pe.wait_ge(v_low, 4 * (c + 1))
                wait(pe, x1_done, 2 * (n - 1) + g + 1)
                for part in range(2):
                    last = nc.tensor.matmul(ps[g][:, :], W_parts[part][:, P * q:P * (q + 1)],
                                            V_parts[slot % 2][:, BANK * g:BANK * (g + 1)],
                                            start=(part == 0), stop=(part == 1))
                last.then_inc(y_done, 1)

            def transpose_x1(n, slot, q, k):
                wait(pe, gx_done, 2 * (n - 1) + k + 1)
                for h in range(CH):
                    last = nc.tensor.transpose(ps[2 + k][:, P * h:P * (h + 1)], x1[slot][:, 2 * q + k, h, :], ident)
                last.then_inc(t_done, 1)

            def convolve(t, g):
                pe.wait_ge(u_done, 2 * t + g + 1)
                wait(pe, r_done, 2 * (t - 1) + g + 1)
                bank = ps[4 + g]
                for m, shift in ((0, 0), (2, 1), (1, 1), (3, 2)):
                    half = m // 2
                    last = nc.tensor.matmul(bank[64 * half:64 * half + 64, :], conv[:, m, :],
                                            u[g][:, :, shift:shift + P], start=(m % 2 == 0) if half == 0 else (m == 2),
                                            stop=(m % 2 == 1))
                last.then_inc(conv_done, 1)

            def transpose_r(t, t_slot, g):
                pe.wait_ge(r_done, 2 * t + g + 1)
                wait(pe, out_done, 2 * (t - 1) + g + 1)
                for b in range(BG):
                    last = nc.tensor.transpose(ps[6 + g][:, P * b:P * (b + 1)],
                                               r[g][t_slot % 2][:, P * b:P * (b + 1)], ident)
                last.then_inc(rt_done, 1)

            def prep_t(n, s):
                slot, q = s // 4, s % 4
                if q == 0:
                    pe.wait_ge(x1_done, 2 * n + 8)
                for k in range(2):
                    transpose_x1(n, slot % 4, q, k)

            pe.wait_ge(w_low, 1)
            pe.wait_ge(v_copied_act, V_ACT * 8)
            pe.wait_ge(v_copied_dve, V_DVE * 8)
            for n in range(9):
                for g in range(G):
                    column_idft(n, n // 4, n // 4, n % 4, g)
                if n >= 4:
                    prep_t(n - 4, n - 4)

            def steps(it):
                known = isinstance(it, int)
                for s in range(STEPS):
                    t = STEPS * it + s
                    slot, q = (s + 9) // 4, (s + 9) % 4
                    for g in range(G):
                        convolve(t, g)
                        if g == 1:
                            transpose_r(t, s, 0)
                        elif not (known and t == 0):
                            transpose_r(t - 1, s - 1, 1)
                        if not (known and t + 9 >= H):
                            column_idft(t + 9, 4 * it + slot, slot, q, g)
                    if not (known and t + 5 >= H):
                        prep_t(t + 5, s + 5)

            pe.wait_ge(conv_in, 16 * 20)
            steps(0)
            with pe.Fori(1, H // STEPS - 1) as it:
                steps(it)
            steps(H // STEPS - 1)
            transpose_r(H - 1, STEPS - 1, 1)

        @block.scalar
        def _(act):
            act.wait_ge(tables_in, 16)
            nc.scalar.activation(W_parts[0][:, :], table("idft_w"), ACT.Copy).then_inc(w_high, 1)

            def squares(b):
                for i in range(TILES):
                    act.wait_ge(tile_in[i % 2], XT_USE * (TILES // 2 * b + i // 2 + 1))
                    flat = tile[i % 2].rearrange("p hh (w c) -> p (hh w) c", c=C)
                    for g in range(SQ_ACT):
                        at = (b * TILES + i) * 16 + g
                        if g == 1:
                            wait(act, squared, 2 * (b * TILES + i))
                        else:
                            wait(act, sq_act, (SQ_ACT - 1) * (b * TILES + i) + max(g - 1, 0))
                        ins = nc.scalar.activation(squares_act[g % 2], flat[:, :, 2 * g:2 * g + 2], ACT.Square,
                                                   accum_out=sq[:, bass.ds(at, 1)])
                        if g < SQ_ACT - 1:
                            ins.then_inc(sq_act, 1)
                        else:
                            ins.then_inc(squared, 2)

            squares(0)
            with act.Fori(1, B) as b:
                squares(b)

            act.wait_ge(var_ready, 1)
            nc.scalar.activation(small[:, 3, :], small[:, 2, :], ACT.Sqrt).then_inc(root_done, 1)

            def evac(s, e):
                act.wait_ge(mix_done, e + s + 1)
                for q in range(4):
                    dst = O_part[32 * q:32 * q + 16, bass.ds(BANK * (e + s), BANK)]
                    last = nc.scalar.activation(dst, ps[4 * s + q][32 * q:32 * q + 16, :], ACT.Copy)
                last.then_inc(o_copied, 1)

            with act.Fori(0, 8) as it:
                for s in range(2):
                    evac(s, 2 * it)

            def spectra_high(c, slot, k):
                if k == 0:
                    wait(act, y_done, 8 * c - 8)
                    act.wait_ge(vc_in[slot % 2], 32 * (slot // 2 + 1) + 16 * (c - slot))
                part = slice(V_PART * k, V_PART * (k + 1))
                nc.scalar.activation(V_parts[slot % 2][:, part], Vc[slot % 2][:, part], ACT.Copy).then_inc(v_high, 1)

            for n in range(8):
                if n >= 2:
                    act.wait_ge(v_stored[n % 2], 32 * (n // 2))
                if n == 7:
                    for c in range(2):
                        for k in range(4):
                            spectra_high(c, c, k)
                for d in range(C):
                    if n == 6 and d == C // 2:
                        act.wait_ge(var_ready, 2)
                        nc.scalar.activation(small[:, 9, :], small[:, 8, :], ACT.Sqrt).then_inc(root_done, 1)
                    if d % 4 == 3:
                        continue
                    act.wait_ge(v_done, C * n + d + 1)
                    nc.scalar.activation(VS[n % 2][:, :, d], ps[d % 4][:, 0:VH], ACT.Copy).then_inc(v_copied_act, 1)

            def relu(t, t_slot, g):
                if isinstance(t, int) and t == H - 1:
                    act.wait_ge(conv_done, 2 * t + g + 1)
                else:
                    act.wait_ge(u_done, 2 * t + g + 3)
                wait(act, rt_done, 2 * (t - 2) + g + 1)
                nc.scalar.activation(r[g][t_slot % 2], ps[4 + g][:, :], ACT.Relu, bias=bias[:, 0:1]).then_inc(r_done, 1)

            def normalise(n, s):
                slot, q = s // 4, s % 4
                if q == 0:
                    wait(act, u_done, 2 * n - 8)
                for k in range(2):
                    b = 2 * q + k
                    act.wait_ge(t_done, 2 * n + k + 1)
                    nc.scalar.activation(gx[slot % 2][:, b], ps[2 + k][:, :].rearrange("p (h j) -> p h j", h=CH),
                                         ACT.Identity, scale=small[:, 11, b:b + 1],
                                         bias=small[:, 13, b:b + 1]).then_inc(gx_done, 1)

            act.wait_ge(norm1_ready, 1)
            act.wait_ge(bias_in, 64)
            for k in range(4):
                spectra_high(2, 2, k)
            for n in range(5):
                if n == 3:
                    spectra_high(3, 3, 0)
                normalise(n, n)

            def steps(it):
                known = isinstance(it, int)
                for s in range(STEPS):
                    t = STEPS * it + s
                    relu(t, s, 0)
                    relu(t, s, 1)
                    if not (known and t + 5 >= H):
                        normalise(t + 5, s + 5)
                    slot, k = (s + 13) // 4, (s + 13) % 4
                    if not (known and 4 * it + slot >= CHUNKS):
                        spectra_high(4 * it + slot, slot, k)

            steps(0)
            with act.Fori(1, H // STEPS - 1) as it:
                steps(it)
            steps(H // STEPS - 1)

        @block.vector
        def _(dve):
            chain = [0]

            def link(ins):
                chain[0] += 1
                ins.then_inc(dve_step, 1)
                dve.wait_ge(dve_step, chain[0])

            dve.wait_ge(tables_in, 16)
            dve.wait_ge(w_high, 1)
            nc.vector.tensor_tensor(W_parts[1][:, :], table("idft_w"), W_parts[0][:, :].bitcast(F32),
                                    ALU.subtract).then_inc(w_low, 1)

            def copy_zt(b, sub, m):
                dve.wait_ge(zt_done, 16 * b + 8 * sub + m + 1)
                wait(dve, coldft_done, 4 * b + 2 * sub + m // 4 - 1)
                nc.vector.tensor_copy(ZT[:, 4 * m:4 * m + 4, :],
                                      ps[4 + m % 2][:, :].rearrange("p (c k) -> p c k", c=4)).then_inc(zt_copied, 1)

            def copy_modes(b, e):
                dve.wait_ge(coldft_done, 4 * b + e + 3)
                dst = X[0:64, bass.ds(b, 1), BANK * e:BANK * (e + 1)].rearrange("p b n -> p (b n)")
                nc.vector.tensor_copy(dst, ps[6 + e][0:64, :]).then_inc(x_copied, 1)

            def behind(b, i, first):
                if first and i < 4:
                    return
                prev, sub = (b - 1, 1) if i < 4 else (b, 0)
                for m in (2 * (i % 4), 2 * (i % 4) + 1):
                    copy_zt(prev, sub, m)
                if not first and i in (3, 5):
                    copy_modes(b - 1, (i - 3) // 2)

            def forward(b, first):
                for i in range(TILES):
                    dve.wait_ge(tile_in[i % 2], XT_USE * (TILES // 2 * b + i // 2 + 1))
                    flat = tile[i % 2].rearrange("p hh (w c) -> p (hh w) c", c=C)
                    for g in range(SQ_ACT, 16):
                        at = (b * TILES + i) * 16 + g
                        v = flat[:, :, 2 * g:2 * g + 2]
                        n = (b * TILES + i) * SQ_DVE + g - SQ_ACT
                        wait(dve, sq_dve, n - 1)
                        nc.vector.scalar_tensor_tensor(squares_dve[g % 2], v, 1.0, v, ALU.mult, ALU.mult,
                                                       accum_out=sq[:, bass.ds(at, 1)]).then_inc(sq_dve, 1)
                    for blk in range(2):
                        dve.wait_ge(rowdft_done, 2 * TILES * b + 2 * i + blk + 1)
                        at = i * TW + 16 * blk
                        nc.vector.tensor_copy(Z[:, :, at:at + 16],
                                              ps[(2 * i + blk) % 4][:, :].rearrange("p (w c) -> p c w", c=C)
                                              ).then_inc(z_copied, 1)
                    behind(b, i, first)

            forward(0, True)
            with dve.Fori(1, B) as b:
                forward(b, False)
            for i in range(4):
                behind(B, i, False)
            copy_modes(B - 1, 1)

            dve.wait_ge(bias_in, 64)
            link(nc.vector.tensor_scalar(neg_bias[:, :], bias[:, :], -1.0, None, ALU.mult))
            dve.wait_ge(squared, 2 * B * TILES)
            dve.wait_ge(sq_act, (SQ_ACT - 1) * B * TILES)
            dve.wait_ge(sq_dve, SQ_DVE * B * TILES)
            nc.vector.tensor_reduce(sumsq[:, :].rearrange("p (b g) -> p b g", b=B),
                                    sq[:, :].rearrange("p (b t g) -> p b g t", b=B, g=16),
                                    AX.X, ALU.add).then_inc(sums_ready, 1)
            dve.wait_ge(sums_done, 1)

            def group_sum(dst, bank, n, mask):
                v = masked[:, 0:B * n].rearrange("p (b g) -> p b g", b=B)
                m = table(mask).rearrange("p (b g) -> p b g", b=1).broadcast_to([P, B, n])
                link(nc.vector.tensor_tensor(v, bank[:, 0:B * n].rearrange("p (b g) -> p b g", b=B), m, ALU.mult))
                link(nc.vector.tensor_reduce(dst, v, AX.X, ALU.add))

            def variance(total, total_sq, mean, var, tmp):
                link(nc.vector.tensor_scalar(mean, total, 1.0 / N2, None, ALU.mult))
                link(nc.vector.tensor_tensor(tmp, mean, mean, ALU.mult))
                link(nc.vector.scalar_tensor_tensor(var, total_sq, 1.0 / N2, tmp, ALU.mult, ALU.subtract))
                nc.vector.tensor_scalar(var, var, 0.0, GN_EPS, ALU.max, ALU.add).then_inc(var_ready, 1)

            def reciprocal_root(var, root, tmp, dst):
                link(nc.vector.reciprocal(tmp, root))
                link(nc.vector.tensor_tensor(tmp, tmp, var, ALU.mult))
                link(nc.vector.tensor_tensor(tmp, tmp, root, ALU.add))
                link(nc.vector.tensor_scalar(tmp, tmp, 0.5, None, ALU.mult))
                link(nc.vector.reciprocal(dst, tmp))

            group_sum(small[:, 0, :], ps[0], 16, "same_group16")
            group_sum(small[:, 1, :], ps[1], 32, "same_group32")
            variance(small[:, 1, :], small[:, 0, :], small[:, 5, :], small[:, 2, :], small[:, 4, :])
            dve.wait_ge(root_done, 1)
            reciprocal_root(small[:, 2, :], small[:, 3, :], small[:, 4, :], small[:, 6, :])
            dve.wait_ge(xc_in, 16 * 8 * (B - 1))
            dve.wait_ge(last_xc_in, 16 * 8)
            zero_mode = XC[0:32, :, 0].rearrange("p (b ri) -> p b ri", ri=2)[:, :, 0]
            link(nc.vector.scalar_tensor_tensor(zero_mode, small[0:32, 1, :], -0.5, zero_mode, ALU.mult, ALU.add))
            for b in range(B):
                ins = nc.vector.tensor_scalar(XC[:, 2 * b:2 * b + 2, :], XC[:, 2 * b:2 * b + 2, :],
                                              small[:, 6, b:b + 1], None, ALU.mult)
            ins.then_inc(xc_scaled, 1)

            def sign_pair(i):
                dve.wait_ge(lv_in[i % 2], 128 * (i // 2 + 1))
                for s in range(2):
                    v = LV[i % 2][64 * s + 32:64 * s + 64, 64 * s:64 * s + 32, :]
                    ins = nc.vector.tensor_scalar(v, v, -1.0, None, ALU.mult)
                ins.then_inc(lv_signed, 1)

            def image_sums(b, step):
                pr = prod[0:64, 0:C * M].rearrange("p (c m) -> p c m", m=M)
                o_t = O[0:64, b].rearrange("p (m c) -> p c m", c=C)
                cs = slice(C * b, C * (b + 1))
                if step == 0:
                    return nc.vector.tensor_tensor(pr, X[0:64, b].rearrange("p (c m) -> p c m", m=M), o_t, ALU.mult)
                if step == 1:
                    return nc.vector.tensor_reduce(R1[0:64, cs], pr, AX.X, ALU.add)
                if step == 2:
                    return nc.vector.tensor_tensor(pr, o_t, o_t, ALU.mult)
                nc.vector.tensor_copy(R3[0:64, cs], pr[:, :, 0])
                return nc.vector.tensor_reduce(R2[0:64, cs], pr, AX.X, ALU.add)

            sign_pair(0)
            sign_pair(1)
            dve.wait_ge(o_in, 32)

            def copy_row_spectra(m, sums):
                if m >= 2:
                    dve.wait_ge(v_stored[m % 2], 32 * (m // 2))
                for d in range(3, C, 4):
                    dve.wait_ge(v_done, C * m + d + 1)
                    nc.vector.tensor_copy(VS[m % 2][:, :, d], ps[3][:, 0:VH]).then_inc(v_copied_dve, 1)
                    if sums:
                        ins = image_sums(2 * m + d // 16, d // 4 % 4)
                        if m == 3 and d == C - 1:
                            ins.then_inc(sums_ready, 1)
                        else:
                            link(ins)

            for m in range(4):
                if m == 3:
                    sign_pair(2)
                copy_row_spectra(m, True)
            copy_row_spectra(4, False)
            sign_pair(3)
            copy_row_spectra(5, False)
            dve.wait_ge(sums_done, 2)
            group_sum(small[:, 7, :], ps[4], 32, "same_group32")
            link(nc.vector.tensor_tensor(small[:, 7, :], small[:, 7, :], small[:, 0, :], ALU.add))
            group_sum(small[:, 10, :], ps[5], 32, "same_group32")
            link(nc.vector.tensor_tensor(small[:, 10, :], small[:, 10, :], small[:, 1, :], ALU.add))
            variance(small[:, 10, :], small[:, 7, :], small[:, 12, :], small[:, 8, :], small[:, 4, :])
            copy_row_spectra(6, False)
            dve.wait_ge(root_done, 2)
            reciprocal_root(small[:, 8, :], small[:, 9, :], small[:, 4, :], small[:, 11, :])
            link(nc.vector.tensor_tensor(small[:, 13, :], small[:, 12, :], small[:, 11, :], ALU.mult))
            link(nc.vector.tensor_scalar(small[:, 13, :], small[:, 13, :], -1.0, bias[:, 0:1], ALU.mult, ALU.add))
            for g in range(G):
                nc.vector.memset(u[g][:, :, 0:1], 0.0)
                ins = nc.vector.memset(u[g][:, :, 129:130], 0.0)
            ins.then_inc(norm1_ready, 1)

            def spectra_low(c, slot, k):
                dve.wait_ge(v_high, 4 * c + k + 1)
                part = slice(V_PART * k, V_PART * (k + 1))
                low = V_parts[slot % 2][64:128, part]
                nc.vector.tensor_tensor(low, Vc[slot % 2][64:128, part], low.bitcast(F32), ALU.subtract).then_inc(v_low, 1)

            for c in range(2):
                for k in range(4):
                    spectra_low(c, c, k)
            copy_row_spectra(7, False)

            def add_y(n, s, it, g):
                slot, q = s // 4, s % 4
                if q == 0 and g == 0:
                    dve.wait_ge(xin_in[slot % 2], 128 * (slot // 2 + 1) + 256 * it)
                    wait(dve, stored[slot % 4], 128 * (slot // 4) + 128 * it)
                dve.wait_ge(y_done, 2 * n + g + 1)
                src = x_in[slot % 2][:, BG * g:BG * (g + 1), :, C * q:C * (q + 1)]
                dst = x1[slot % 4][:, BG * g:BG * (g + 1), :, C * q:C * (q + 1)]
                y = ps[g][:, :].rearrange("p (b h c) -> p b h c", b=BG, h=CH)
                nc.vector.tensor_tensor(dst, y, src, ALU.add).then_inc(x1_done, 1)

            def next_u(t, s, g):
                slot, row = (s + 1) // 4, (s + 1) % 4
                dve.wait_ge(conv_done, 2 * t + g + 1)
                if row == 0:
                    dve.wait_ge(gx_done, 2 * (t + 1) + 4 * g + 4)
                nc.vector.scalar_tensor_tensor(
                    u[g][:, :, 1:129], ps[4 + g][:, :].rearrange("p (b j) -> p b j", b=BG), neg_bias[:, 0:1],
                    gx[slot % 2][:, BG * g:BG * (g + 1), row, :], ALU.max, ALU.add).then_inc(u_done, 1)

            def add_r(t, s, g):
                dve.wait_ge(rt_done, 2 * t + g + 1)
                v = x1[s // 4 % 4][:, BG * g:BG * (g + 1), s % 4, :]
                nc.vector.tensor_tensor(v, ps[6 + g][:, :].rearrange("p (b n) -> p b n", b=BG), v,
                                        ALU.add).then_inc(out_done, 1)

            for n in range(9):
                if n == 0:
                    dve.wait_ge(v_stored[0], 4 * 32)
                if n == 8:
                    dve.wait_ge(v_stored[1], 4 * 32)
                    for k in range(4):
                        spectra_low(2, 2, k)
                for g in range(G):
                    add_y(n, n, 0, g)
            spectra_low(3, 3, 0)
            for g in range(G):
                dve.wait_ge(gx_done, 4 * g + 4)
                nc.vector.tensor_scalar(u[g][:, :, 1:129], gx[0][:, BG * g:BG * (g + 1), 0, :],
                                        bias[:, 0:1], None, ALU.subtract).then_inc(u_done, 1)

            def steps(it):
                known = isinstance(it, int)
                for s in range(STEPS):
                    t = STEPS * it + s
                    for g in range(G):
                        if not (known and t + 1 >= H):
                            next_u(t, s, g)
                        if g == 1:
                            add_r(t, s, 0)
                        elif not (known and t == 0):
                            add_r(t - 1, s + STEPS - 1, 1)
                        if not (known and t + 9 >= H):
                            add_y(t + 9, s + 9, it, g)
                    slot, k = (s + 13) // 4, (s + 13) % 4
                    if not (known and 4 * it + slot >= CHUNKS):
                        spectra_low(4 * it + slot, slot, k)

            steps(0)
            with dve.Fori(1, H // STEPS - 1) as it:
                steps(it)
            steps(H // STEPS - 1)
            add_r(H - 1, STEPS - 1, 1)


_INS = ["x", "L0_conv_W", "L1_conv_w", "L1_conv_b"]


def kernel(**inputs):
    import numpy as _np
    import concourse.bacc as _bacc
    from concourse import mybir as _mybir
    from concourse.bass_utils import run_bass_kernel_spmd as _run

    nc = _bacc.Bacc("TRN2", target_bir_lowering=False, num_devices=1)
    shape = inputs["x"].shape
    arrays, args = {}, []
    named = [(name, _np.ascontiguousarray(inputs[name])) for name in _INS]
    for name, a in named + [("tables", tables(shape[1], shape[2]))]:
        arrays[f"in_{name}_dram"] = a
        args.append(nc.dram_tensor(f"in_{name}_dram", a.shape, _mybir.dt.from_np(a.dtype), kind="ExternalInput").ap())
    args.append(nc.dram_tensor("out_0_dram", shape, _mybir.dt.float32, kind="ExternalOutput").ap())
    conv_preact_pair(nc, *args)
    r = _run(nc, [arrays], core_ids=[0])
    return r.results[0]["out_0_dram"]
```
